# Optimizing a Trainium2 kernel written in Bass

```python
import numpy as np
import jax
import jax.numpy as jnp

def _softmax(x, axis=-1):
    return jax.nn.softmax(x, axis=axis)

def _gelu(x):
    return jax.nn.gelu(x, approximate=True)

def _silu(x):
    return jax.nn.silu(x)

def _sigmoid(x):
    return jax.nn.sigmoid(x)

def _layernorm(x, axis=-1, eps=1e-05):
    m = jnp.mean(x, axis=axis, keepdims=True)
    v = jnp.var(x, axis=axis, keepdims=True)
    return (x - m) / jnp.sqrt(v + eps)

def _scatter_add(tgt, idx, src, axis=0):
    return tgt.at[idx].add(src)

def _segment_sum(src, seg, n):
    return jax.ops.segment_sum(src, seg, n)
kernel_name = 'mk_xattn_ffn_d2_seqx_r4_4ee9bc'

def setup_inputs(seed: int=0):
    np.random.seed(seed)
    _w = jnp.asarray

    def _rec_inputs():
        import jax
        import jax.numpy as jnp
        _rk = jax.random.key(seed)
        x = -0.0002928 + 1 * jax.random.normal(jax.random.fold_in(_rk, 1), (32, 128, 256), jnp.float32)
        _lenS = 128 - jax.random.randint(jax.random.fold_in(_rk, 7), (32,), 0, max(1, 128 // 4) + 1, jnp.int32)
        _lenS2 = 128 - jax.random.randint(jax.random.fold_in(_rk, 8), (32,), 0, max(1, 128 // 4) + 1, jnp.int32)
        _ctx_1024P = jax.random.normal(jax.random.fold_in(_rk, 11), (32, 16, 256), jnp.float32)
        _ctx_1024c = jax.random.dirichlet(jax.random.fold_in(_rk, 511), 0.3 * jnp.ones((16,), jnp.float32), (32, 128))
        _ctx_1024t = jnp.einsum('bsk,bkd->bsd', _ctx_1024c, _ctx_1024P)
        _ctx_1024t = _ctx_1024t * jax.lax.rsqrt(jnp.mean(jnp.square(_ctx_1024t)) + 1e-12) * 0.953939
        ctx_1024 = -1.39393e-06 + 0.999914 * (_ctx_1024t + 0.3 * jax.random.normal(jax.random.fold_in(_rk, 611), (32, 128, 256), jnp.float32))
        _validS = jnp.arange(128)[None, :] < _lenS[:, None]
        _validS2 = jnp.arange(128)[None, :] < _lenS2[:, None]
        _causal = jnp.tril(jnp.ones((128, 128), dtype=bool))
        mask_1x1xSxS2_fk1 = jnp.where(jnp.broadcast_to(_validS2[0:1, None, None, :], (1, 1, 128, 128)), 1.0, 0.0).astype(jnp.float32)
        return (x, ctx_1024, mask_1x1xSxS2_fk1)
    x, ctx_1024, mask_1x1xSxS2_fk1 = _rec_inputs()

    def _L0_xattn_setup():
        import jax, jax.numpy as jnp
        import numpy as np
        B, S, D_MODEL, H = (2, 512, 256, 16)
        D_H = D_MODEL // H

        def _split_heads(x):
            b, s, _ = x.shape
            return x.reshape(b, s, H, D_H).transpose(0, 2, 1, 3)
        key = jax.random.key(seed)
        ks = jax.random.split(key, 12)
        std = 1.0 / np.sqrt(D_MODEL)
        inp = {'query': jax.random.normal(ks[0], (B, S, D_MODEL), jnp.float32), 'key': jax.random.normal(ks[1], (B, S, D_MODEL), jnp.float32), 'value': jax.random.normal(ks[2], (B, S, D_MODEL), jnp.float32), 'mask': jnp.triu(jnp.ones((S, S), jnp.float32), k=1)[None, None], 'Wq': jax.random.normal(ks[3], (D_MODEL, D_MODEL), jnp.float32) * std, 'bq': jnp.zeros((D_MODEL,), jnp.float32), 'Wk': jax.random.normal(ks[4], (D_MODEL, D_MODEL), jnp.float32) * std, 'bk': jnp.zeros((D_MODEL,), jnp.float32), 'Wv': jax.random.normal(ks[5], (D_MODEL, D_MODEL), jnp.float32) * std, 'bv': jnp.zeros((D_MODEL,), jnp.float32), 'Wo': jax.random.normal(ks[6], (D_MODEL, D_MODEL), jnp.float32) * std, 'bo': jnp.zeros((D_MODEL,), jnp.float32)}
        return inp
    _L0_xattn_all = _L0_xattn_setup()
    _L0_xattn_in = {k: v for k, v in _L0_xattn_all.items() if k in ('Wq', 'bq', 'Wk', 'bk', 'Wv', 'bv', 'Wo', 'bo')}
    del _L0_xattn_all

    def _L0_ffn_setup():
        import jax, jax.numpy as jnp
        import numpy as np
        B, S, D, F, E, K = (4, 512, 256, 1024, 4, 2)
        key = jax.random.key(seed)
        k = jax.random.split(key, 6)
        x = jax.random.normal(k[0], (B, S, D), jnp.float32)
        router_w = jax.random.normal(k[1], (D, E), jnp.float32) * D ** (-0.5)
        router_b = jnp.zeros((E,), jnp.float32)
        w1 = jax.random.normal(k[2], (E, D, F), jnp.float32) * 0.02
        w3 = jax.random.normal(k[3], (E, D, F), jnp.float32) * 0.02
        w2 = jax.random.normal(k[4], (E, F, D), jnp.float32) * 0.02
        return {'x': x, 'router_w': router_w, 'router_b': router_b, 'w1': w1, 'w3': w3, 'w2': w2}
    _L0_ffn_all = _L0_ffn_setup()
    _L0_ffn_in = {k: v for k, v in _L0_ffn_all.items() if k in ('router_w', 'router_b', 'w1', 'w3', 'w2')}
    del _L0_ffn_all

    def _L1_xattn_setup():
        import jax, jax.numpy as jnp
        import numpy as np
        D_MODEL = 256
        NUM_HEADS = 16
        EPS = 1e-05

        def _layernorm(x, gamma, beta):
            mu = jnp.mean(x, axis=-1, keepdims=True)
            var = jnp.mean(jnp.square(x - mu), axis=-1, keepdims=True)
            return (x - mu) * jax.lax.rsqrt(var + EPS) * gamma + beta
        key = jax.random.key(seed)
        ks = jax.random.split(key, 8)
        B, S, D = (4, 512, D_MODEL)
        xav = (6.0 / (D + D)) ** 0.5
        inp = {'q': jax.random.normal(ks[0], (B, S, D), dtype=jnp.float32), 'k': jax.random.normal(ks[1], (B, S, D), dtype=jnp.float32), 'v': jax.random.normal(ks[2], (B, S, D), dtype=jnp.float32), 'Wq': jax.random.uniform(ks[3], (D, D), jnp.float32, -xav, xav), 'Wk': jax.random.uniform(ks[4], (D, D), jnp.float32, -xav, xav), 'Wv': jax.random.uniform(ks[5], (D, D), jnp.float32, -xav, xav), 'Wo': jax.random.uniform(ks[6], (D, D), jnp.float32, -xav, xav), 'bo': jnp.zeros((D,), jnp.float32), 'q_gamma': jnp.ones((D,), jnp.float32), 'q_beta': jnp.zeros((D,), jnp.float32), 'k_gamma': jnp.ones((D,), jnp.float32), 'k_beta': jnp.zeros((D,), jnp.float32)}
        return inp
    _L1_xattn_all = _L1_xattn_setup()
    _L1_xattn_in = {k: v for k, v in _L1_xattn_all.items() if k in ('Wq', 'Wk', 'Wv', 'Wo', 'bo', 'q_gamma', 'q_beta', 'k_gamma', 'k_beta')}
    del _L1_xattn_all

    def _L1_ffn_setup():
        import jax, jax.numpy as jnp
        import numpy as np
        EPS = 1e-05
        LN_EPS = 1e-05
        NUM_EXPERTS = 8
        TOP_K = 2
        HIDDEN = 256
        INTER = 512

        def _swiglu(x, wg, wu, wd):
            return jax.nn.silu(x @ wg) * (x @ wu) @ wd
        key = jax.random.key(seed)
        ks = jax.random.split(key, 10)
        B, S, H, I, E = (8, 1024, HIDDEN, INTER, NUM_EXPERTS)
        std_h = 1.0 / np.sqrt(H)
        std_i = 1.0 / np.sqrt(I)
        return {'x': jax.random.normal(ks[0], (B, S, H), dtype=jnp.float32), 'ln_scale': jnp.ones((H,), dtype=jnp.float32), 'ln_bias': jnp.zeros((H,), dtype=jnp.float32), 'gate_w': jax.random.normal(ks[1], (E, H), dtype=jnp.float32) * 0.01, 'Wg': jax.random.normal(ks[2], (E, H, I), dtype=jnp.float32) * std_h, 'Wu': jax.random.normal(ks[3], (E, H, I), dtype=jnp.float32) * std_h, 'Wd': jax.random.normal(ks[4], (E, I, H), dtype=jnp.float32) * std_i, 'sWg': jax.random.normal(ks[5], (H, I), dtype=jnp.float32) * std_h, 'sWu': jax.random.normal(ks[6], (H, I), dtype=jnp.float32) * std_h, 'sWd': jax.random.normal(ks[7], (I, H), dtype=jnp.float32) * std_i}
    _L1_ffn_all = _L1_ffn_setup()
    _L1_ffn_in = {k: v for k, v in _L1_ffn_all.items() if k in ('ln_scale', 'ln_bias', 'gate_w', 'Wg', 'Wu', 'Wd', 'sWg', 'sWu', 'sWd')}
    del _L1_ffn_all
    return {'x': x, 'ctx_1024': ctx_1024, 'mask_1x1xSxS2_fk1': mask_1x1xSxS2_fk1, 'L0_xattn_Wq': _L0_xattn_in['Wq'], 'L0_xattn_bq': _L0_xattn_in['bq'], 'L0_xattn_Wk': _L0_xattn_in['Wk'], 'L0_xattn_bk': _L0_xattn_in['bk'], 'L0_xattn_Wv': _L0_xattn_in['Wv'], 'L0_xattn_bv': _L0_xattn_in['bv'], 'L0_xattn_Wo': _L0_xattn_in['Wo'], 'L0_xattn_bo': _L0_xattn_in['bo'], 'L0_ffn_router_w': _L0_ffn_in['router_w'], 'L0_ffn_router_b': _L0_ffn_in['router_b'], 'L0_ffn_w1': _L0_ffn_in['w1'], 'L0_ffn_w3': _L0_ffn_in['w3'], 'L0_ffn_w2': _L0_ffn_in['w2'], 'L1_xattn_Wq': _L1_xattn_in['Wq'], 'L1_xattn_Wk': _L1_xattn_in['Wk'], 'L1_xattn_Wv': _L1_xattn_in['Wv'], 'L1_xattn_Wo': _L1_xattn_in['Wo'], 'L1_xattn_bo': _L1_xattn_in['bo'], 'L1_xattn_q_gamma': _L1_xattn_in['q_gamma'], 'L1_xattn_q_beta': _L1_xattn_in['q_beta'], 'L1_xattn_k_gamma': _L1_xattn_in['k_gamma'], 'L1_xattn_k_beta': _L1_xattn_in['k_beta'], 'L1_ffn_ln_scale': _L1_ffn_in['ln_scale'], 'L1_ffn_ln_bias': _L1_ffn_in['ln_bias'], 'L1_ffn_gate_w': _L1_ffn_in['gate_w'], 'L1_ffn_Wg': _L1_ffn_in['Wg'], 'L1_ffn_Wu': _L1_ffn_in['Wu'], 'L1_ffn_Wd': _L1_ffn_in['Wd'], 'L1_ffn_sWg': _L1_ffn_in['sWg'], 'L1_ffn_sWu': _L1_ffn_in['sWu'], 'L1_ffn_sWd': _L1_ffn_in['sWd']}

def reference(x, ctx_1024, mask_1x1xSxS2_fk1, L0_xattn_Wq, L0_xattn_bq, L0_xattn_Wk, L0_xattn_bk, L0_xattn_Wv, L0_xattn_bv, L0_xattn_Wo, L0_xattn_bo, L0_ffn_router_w, L0_ffn_router_b, L0_ffn_w1, L0_ffn_w3, L0_ffn_w2, L1_xattn_Wq, L1_xattn_Wk, L1_xattn_Wv, L1_xattn_Wo, L1_xattn_bo, L1_xattn_q_gamma, L1_xattn_q_beta, L1_xattn_k_gamma, L1_xattn_k_beta, L1_ffn_ln_scale, L1_ffn_ln_bias, L1_ffn_gate_w, L1_ffn_Wg, L1_ffn_Wu, L1_ffn_Wd, L1_ffn_sWg, L1_ffn_sWu, L1_ffn_sWd):
    import jax
    import jax.numpy as jnp

    def _L0_xattn_ref(query, key, value, mask, Wq, bq, Wk, bk, Wv, bv, Wo, bo):
        import jax, jax.numpy as jnp
        import numpy as np
        B, S, D_MODEL, H = (2, 512, 256, 16)
        D_H = D_MODEL // H

        def _split_heads(x):
            b, s, _ = x.shape
            return x.reshape(b, s, H, D_H).transpose(0, 2, 1, 3)
        q = _split_heads(query @ Wq + bq)
        k = _split_heads(key @ Wk + bk)
        v = _split_heads(value @ Wv + bv)
        scale = jnp.sqrt(jnp.asarray(D_H, jnp.float32))
        scores = jnp.einsum('bhqd,bhkd->bhqk', q, k) / scale
        scores = scores + mask * -1000000000.0
        attn = jax.nn.softmax(scores, axis=-1)
        out = jnp.einsum('bhqk,bhkd->bhqd', attn, v)
        out = out.transpose(0, 2, 1, 3).reshape(query.shape[0], -1, D_MODEL)
        return out @ Wo + bo

    def _L0_ffn_ref(x, router_w, router_b, w1, w3, w2):
        import jax, jax.numpy as jnp
        import numpy as np
        B, S, D, F, E, K = (4, 512, 256, 1024, 4, 2)
        b, s, d = x.shape
        T = b * s
        e = router_w.shape[1]
        xf = x.reshape(T, d)
        logits = xf @ router_w + router_b
        probs = jax.nn.softmax(logits, axis=-1)
        top_p, top_i = jax.lax.top_k(probs, K)
        top_p = top_p / jnp.sum(top_p, axis=-1, keepdims=True)
        gates = jnp.zeros((T, e), xf.dtype).at[jnp.arange(T)[:, None], top_i].add(top_p)
        h = jax.nn.silu(jnp.einsum('td,edf->etf', xf, w1)) * jnp.einsum('td,edf->etf', xf, w3)
        expert_out = jnp.einsum('etf,efd->etd', h, w2)
        out = jnp.einsum('te,etd->td', gates, expert_out)
        return out.reshape(b, s, d)

    def _L1_xattn_ref(q, k, v, Wq, Wk, Wv, Wo, bo, q_gamma, q_beta, k_gamma, k_beta):
        import jax, jax.numpy as jnp
        import numpy as np
        D_MODEL = 256
        NUM_HEADS = 16
        EPS = 1e-05

        def _layernorm(x, gamma, beta):
            mu = jnp.mean(x, axis=-1, keepdims=True)
            var = jnp.mean(jnp.square(x - mu), axis=-1, keepdims=True)
            return (x - mu) * jax.lax.rsqrt(var + EPS) * gamma + beta
        B, S, D = q.shape
        H = NUM_HEADS
        scale = 1.0 / D ** 0.5
        qp = _layernorm(q @ Wq, q_gamma, q_beta)
        kp = _layernorm(k @ Wk, k_gamma, k_beta)
        vp = v @ Wv
        qh = qp.reshape(B, S, H, D // H)
        kh = kp.reshape(B, S, H, D // H)
        vh = vp.reshape(B, S, H, D // H)
        attn = jnp.einsum('bqhd,bkhd->bhqk', qh, kh) * scale
        attn = jax.nn.softmax(attn, axis=-1)
        x = jnp.einsum('bhqk,bkhd->bqhd', attn, vh).reshape(B, S, D)
        return x @ Wo + bo

    def _L1_ffn_ref(x, ln_scale, ln_bias, gate_w, Wg, Wu, Wd, sWg, sWu, sWd):
        import jax, jax.numpy as jnp
        import numpy as np
        EPS = 1e-05
        LN_EPS = 1e-05
        NUM_EXPERTS = 8
        TOP_K = 2
        HIDDEN = 256
        INTER = 512

        def _swiglu(x, wg, wu, wd):
            return jax.nn.silu(x @ wg) * (x @ wu) @ wd
        B, S, H = x.shape
        xf = x.reshape(-1, H)
        mu = jnp.mean(xf, axis=-1, keepdims=True)
        var = jnp.var(xf, axis=-1, keepdims=True)
        xn = (xf - mu) * jax.lax.rsqrt(var + LN_EPS) * ln_scale + ln_bias
        logits = xn @ gate_w.T
        probs = jax.nn.softmax(logits, axis=-1)
        tk_probs, tk_idx = jax.lax.top_k(probs, TOP_K)
        tk_probs = tk_probs / (jnp.sum(tk_probs, axis=-1, keepdims=True) + EPS)
        onehot = tk_idx[..., None] == jnp.arange(NUM_EXPERTS)[None, None, :]
        w = jnp.sum(tk_probs[..., None] * onehot.astype(tk_probs.dtype), axis=1)
        out = _swiglu(xf, sWg, sWu, sWd)
        for e in range(NUM_EXPERTS):
            out = out + w[:, e:e + 1] * _swiglu(xf, Wg[e], Wu[e], Wd[e])
        return out.reshape(B, S, H)
    x = x + _L0_xattn_ref(_layernorm(x, axis=-1), ctx_1024, ctx_1024, mask_1x1xSxS2_fk1, L0_xattn_Wq, L0_xattn_bq, L0_xattn_Wk, L0_xattn_bk, L0_xattn_Wv, L0_xattn_bv, L0_xattn_Wo, L0_xattn_bo)
    x = x + _L0_ffn_ref(_layernorm(x, axis=-1), L0_ffn_router_w, L0_ffn_router_b, L0_ffn_w1, L0_ffn_w3, L0_ffn_w2)
    x = x + _L1_xattn_ref(_layernorm(x, axis=-1), ctx_1024, ctx_1024, L1_xattn_Wq, L1_xattn_Wk, L1_xattn_Wv, L1_xattn_Wo, L1_xattn_bo, L1_xattn_q_gamma, L1_xattn_q_beta, L1_xattn_k_gamma, L1_xattn_k_beta)
    x = x + _L1_ffn_ref(_layernorm(x, axis=-1), L1_ffn_ln_scale, L1_ffn_ln_bias, L1_ffn_gate_w, L1_ffn_Wg, L1_ffn_Wu, L1_ffn_Wd, L1_ffn_sWg, L1_ffn_sWu, L1_ffn_sWd)
    return x

_drawn_inputs = setup_inputs


def setup_inputs(seed=0):
    import zlib

    import numpy as np

    out = dict(_drawn_inputs(seed))
    spreads = {'L0_xattn_bq': (0.0, 0.1),
     'L0_xattn_bk': (0.0, 0.1),
     'L0_xattn_bv': (0.0, 0.1),
     'L0_xattn_bo': (0.0, 0.1),
     'L0_ffn_router_b': (0.0, 2.0),
     'L1_xattn_bo': (0.0, 0.1),
     'L1_xattn_q_gamma': (1.0, 0.6),
     'L1_xattn_q_beta': (0.0, 0.444),
     'L1_xattn_k_gamma': (1.0, 0.6),
     'L1_xattn_k_beta': (0.0, 2.0),
     'L1_ffn_ln_scale': (1.0, 0.2),
     'L1_ffn_ln_bias': (0.0, 0.1)}
    factors = {}
    for name, (base, spread) in spreads.items():
        noise = np.random.default_rng([zlib.crc32(name.encode()), seed]).standard_normal(out[name].shape)
        drawn = base * np.exp(spread * noise) if base else spread * noise
        out[name] = jnp.asarray(drawn.astype(out[name].dtype))
    for name, factor in factors.items():
        out[name] = (out[name] * factor).astype(out[name].dtype)
    return out
```

```python
from contextlib import ExitStack

import concourse.bass as bass
from concourse import mybir

F32 = mybir.dt.float32
ALU = mybir.AluOpType
ACT = mybir.ActivationFunctionType
AX = mybir.AxisListType

P = 128
D = 256
KC = D // P
H = 16
DH = D // H
EPS = 1e-5
GRP = 32
PAR = 2
NJ = P // GRP
QROW = D + DH
VROW = DH + 1
BANK = 512


def wait(eng, sem, value):
    if isinstance(value, int) and value <= 0:
        return
    eng.wait_ge(sem, value)


def over_tiles(eng, n, body, extra=1):
    first, turns = 4, n // 2 - 1
    for i in range(first):
        body(i, i % 2)
    with eng.Fori(first // 2, turns) as turn:
        for p in (0, 1):
            body(2 * turn + p, p)
    for i in range(2 * turns, n + extra):
        body(i, i % 2)


def within(i, low, high):
    return not isinstance(i, int) or low <= i < high


class Core:

    def __init__(self, nc, stack):
        self.nc, self.stack = nc, stack

    def expert_views(self, moe):
        n = moe.E * moe.F * KC
        g, u = (self.W[:, a, 0:n].rearrange("p (e c f) -> p e c f", e=moe.E, c=KC) for a in (0, 1))
        return g, u, self.W[:, 2, 0:n].rearrange("p (e c d) -> p e c d", e=moe.E, d=D)

    def phase_sems(self, ctx, prefix):
        taken = []

        def clear():
            with self.nc.Block() as block:

                @block.gpsimd
                def _(pool):
                    for s in taken:
                        pool.sem_clear(s)

        def sem(name):
            taken.append(sems.enter_context(self.nc.semaphore(prefix + name)))
            return taken[-1]

        sems = ctx.enter_context(ExitStack())
        ctx.callback(clear)
        return sem

    def sem(self, name):
        return self.stack.enter_context(self.nc.semaphore(name))

    def sb(self, name, shape, stack=None, dt=F32):
        return (stack or self.stack).enter_context(self.nc.sbuf_tensor(name, shape, dt))


def load_constants(core, io):
    nc = core.nc
    zeroed, ready = core.sem("ident_zeroed"), core.sem("constants_ready")
    with nc.Block() as block:

        @block.sync
        def _(sp):
            nt = core.X.shape[1]
            for c in range(4):
                part = slice(c * nt // 4, (c + 1) * nt // 4)
                sp.dma_start(core.X[:, part, :],
                             io["x"][part].rearrange("t p d -> p t d")).then_inc(core.x_loaded, 16)

        @block.gpsimd
        def _(pool):
            pool.memset(core.ident[:], 0.0).then_inc(zeroed, 1)
            pool.wait_ge(zeroed, 1)
            pool.affine_select(out=core.ident[:], in_=core.ident[:], compare_op=ALU.not_equal, fill=1.0,
                               base=0, pattern=[[-1, P]], channel_multiplier=1).then_inc(ready, 1)
            pool.memset(core.minus_half[:], -0.5).then_inc(ready, 1)
            pool.memset(core.eps[:], EPS).then_inc(ready, 1)
            pool.memset(core.zeros[:], 0.0).then_inc(ready, 1)
            for c in range(4):
                pool.wait_ge(core.x_loaded, 16 * (c + 1))
            pool.wait_ge(ready, 4)


def attention(core, io, layer, nt, moe):
    nc = core.nc
    first = layer == 0
    N = f"a{layer}_"
    X, ident = core.X, core.ident
    with ExitStack() as ctx:
        sem = core.phase_sems(ctx, N)
        sb = lambda name, shape: core.sb(N + name, shape, ctx)
        wq, wk, wv, wo = (sb(w, [P, KC, D]) for w in ("wq", "wk", "wv", "wo"))
        rows = ["bq", "bk", "bv", "bo"] if first else ["bo", "q_gamma", "q_beta", "k_gamma", "k_beta"]
        vec = {r: sb(r, [P, D]) for r in rows}
        ctx_sb = sb("ctx", [P, 2, D])
        xn = sb("xn", [P, 2, D])
        T1s = sb("ctxT_xnT", [P, 4, P])
        qpad = sb("qpad", [P, PAR * QROW])
        ksb = sb("ksb", [P, D])
        vsb = sb("vsb", [P, 2, H, VROW])
        qT = sb("qT", [P, PAR * KC, P])
        kT = sb("kT", [P, KC, P])
        SM = sb("scores", [P, 2, NJ, BANK])
        mx = sb("mx", [P, 2, H])
        PTs = sb("weightsT", [P, 2, BANK])
        rsum = sb("rsum", [P, H])
        osb = sb("osb", [P, D])
        oT = sb("oT", [P, KC, P])
        delta = sb("delta", [P, D])
        xst, xmv, xrs = sb("xst", [P, 2, 6]), sb("xmv", [P, 2, 2]), sb("xrs", [P, 2, 2])
        if first:
            mask = sb("mask", [P, P])
        else:
            qkst, qkmv, qkrs = sb("qkst", [P, 2, 6]), sb("qkmv", [P, 2, 2]), sb("qkrs", [P, 2, 2])
            qkn = sb("qkn", [P, 2, D])

        Sps = [core.bank[j] for j in range(NJ)]
        PTps = [core.bank[4], core.bank[5]]
        G, O = core.bank[6], core.bank[7]

        def heads_of(j):
            return [(c, par, c * 8 + j * PAR + par) for c in range(KC) for par in range(PAR)]

        q_odd_even = qpad[:].rearrange("p (r w) -> p r w", r=PAR)[:, :, 0:D].rearrange(
            "p r (m w) -> p r m w", w=PAR * DH)[:, :, :, 0:DH]

        def as_parity(ap):
            return ap.rearrange("p (m r w) -> p r m w", r=PAR, w=DH)

        w_loaded, vec_loaded, init = sem("w_loaded"), sem("vec_loaded"), sem("buffers_set")
        ctx_loaded = [sem("ctx_loaded0"), sem("ctx_loaded1")]
        x_mv, x_var, x_rstd, xn_ready = (sem(s) for s in ("x_mv", "x_var", "x_rstd", "xn_ready"))
        t1_done, t1_copied = sem("t1_done"), sem("t1_copied")
        qk_done, qk_copied, qk_ready = sem("qk_done"), sem("qk_copied"), sem("qk_ready")
        v_done, v_copied = sem("v_done"), sem("v_copied")
        qt_done, qt_copied, kt_done, kt_copied = (sem(s) for s in ("qt_done", "qt_copied", "kt_done", "kt_copied"))
        s_done, s_copied, mx_ready, shifted, probs = (sem(s) for s in ("s_done", "s_copied", "mx_ready", "shifted", "probs"))
        pt_done, pt_copied, av_done = sem("pt_done"), sem("pt_copied"), sem("av_done")
        rsum_ready, o_ready, ot_done, ot_copied = (sem(s) for s in ("rsum_ready", "o_ready", "ot_done", "ot_copied"))
        op_done, d_ready, x_updated = sem("op_done"), sem("d_ready"), sem("x_updated")
        if not first:
            qk_mv, qk_var, qk_rstd, qk_norm, qk_scaled = (
                sem(s) for s in ("qk_mv", "qk_var", "qk_rstd", "qk_norm", "qk_scaled"))

        block = ctx.enter_context(nc.Block())

        @block.sync
        def _(sp):
            for dst, name in ((wq, "Wq"), (wk, "Wk"), (wv, "Wv"), (wo, "Wo")):
                sp.dma_start(dst[:], io[f"L{layer}_xattn_{name}"].rearrange("(c p) n -> p c n", p=P)
                             ).then_inc(w_loaded, 16)
            for r in rows:
                sp.dma_start(vec[r][:], io[f"L{layer}_xattn_{r}"].partition_broadcast(P)).then_inc(vec_loaded, 16)
            if first:
                sp.dma_start(mask[:], io["mask_1x1xSxS2_fk1"].rearrange("a b q k -> (a b q) k")
                             ).then_inc(vec_loaded, 16)

            def body(t, p):
                if not within(t, 0, nt):
                    return
                wait(sp, t1_done, t - 1)
                sp.dma_start(ctx_sb[:, p, :], io["ctx_1024"][t]).then_inc(ctx_loaded[p], 16)
                if isinstance(t, int) and t == 1:
                    load_experts(core, moe, sp)
                    sp.dma_start(core.slots_in[layer].rearrange("(s p) d -> p s d", p=P),
                                 core.zeros[:].unsqueeze(1).broadcast_to([P, moe.tiles, D])).then_inc(core.zeroed[layer], 16)
            over_tiles(sp, nt, body)

        nvec = 16 * (len(rows) + (1 if first else 0))

        @block.gpsimd
        def _(pool):
            pool.memset(qpad[:], 0.0).then_inc(init, 1)
            pool.memset(vsb[:], 1.0).then_inc(init, 1)
            if not first:
                pool.wait_ge(vec_loaded, nvec)

            def x_std(t, p):
                pool.wait_ge(x_mv, t + 1)
                pool.tensor_tensor(xrs[:, p, 0:1], xmv[:, p, 1:2], core.eps[:], ALU.add).then_inc(x_var, 1)
                pool.wait_ge(x_var, t + 1)
                pool.tensor_tensor(xrs[:, p, 1:2], xrs[:, p, 0:1], core.minus_half[:, 0:1],
                                   ALU.pow).then_inc(x_rstd, 1)

            def shift(t, p):
                pool.wait_ge(mx_ready, t + 1)
                for j in range(NJ):
                    s = SM[:, p, j, :].rearrange("p (h k) -> p h k", h=4)
                    m = mx[:, p, 4 * j:4 * j + 4].unsqueeze(2).broadcast_to([P, 4, P])
                    pool.tensor_tensor(s, s, m, ALU.subtract).then_inc(shifted, 1)

            def qk_affine(t):
                pool.wait_ge(qk_mv, t + 1)
                pool.tensor_tensor(qkrs[:, 0, :], qkmv[:, :, 1], core.eps[:].broadcast_to([P, 2]), ALU.add).then_inc(qk_var, 1)
                pool.wait_ge(qk_var, t + 1)
                pool.tensor_tensor(qkrs[:, 1, :], qkrs[:, 0, :], core.minus_half[:, 0:2],
                                   ALU.pow).then_inc(qk_rstd, 1)
                pool.wait_ge(qk_norm, 2 * (t + 1))
                pool.tensor_tensor(qkn[:, 0, :], qkn[:, 0, :], vec["q_gamma"][:], ALU.mult).then_inc(qk_scaled, 1)
                pool.tensor_tensor(qkn[:, 1, :], qkn[:, 1, :], vec["k_gamma"][:], ALU.mult).then_inc(qk_scaled, 1)
                wait(pool, qt_done, t)
                wait(pool, kt_done, t)
                pool.wait_ge(qk_scaled, 2 * t + 1)
                pool.wait_ge(init, 2)
                for r in range(PAR):
                    pool.tensor_tensor(q_odd_even[:, r], as_parity(qkn[:, 0, :])[:, r],
                                       as_parity(vec["q_beta"][:])[:, r], ALU.add).then_inc(qk_ready, 1)
                pool.wait_ge(qk_scaled, 2 * t + 2)
                pool.tensor_tensor(ksb[:], qkn[:, 1, :], vec["k_beta"][:], ALU.add).then_inc(qk_ready, 1)

            x_std(0, 0)
            x_std(1, 1)
            if not first:
                qk_affine(0)

            def body(i, p):
                if within(i, 0, nt - 2):
                    x_std(i + 2, p)
                if first:
                    if within(i, 0, nt):
                        shift(i, p)
                elif within(i, 0, nt - 1):
                    qk_affine(i + 1)
            over_tiles(pool, nt, body)

        @block.vector
        def _(dve):
            def x_stats(t, p):
                wait(dve, x_rstd, t - 1)
                wait(dve, xn_ready, t - 1)
                wait(dve, x_mv, t - 1)
                dve.bn_stats(xst[:, p, :], X[:, t, :])
                dve.drain()
                dve.bn_aggr(xmv[:, p, :], xst[:, p, :]).then_inc(x_mv, 1)

            def x_norm(t, p):
                dve.wait_ge(x_rstd, t + 1)
                wait(dve, t1_done, t - 1)
                dve.tensor_scalar(xn[:, p, :], X[:, t, :], xmv[:, p, 0:1], xrs[:, p, 1:2],
                                  ALU.subtract, ALU.mult).then_inc(xn_ready, 1)

            def qk_evacuate(t):
                dve.wait_ge(qk_done, t + 1)
                wait(dve, qt_done, t)
                wait(dve, kt_done, t)
                dve.tensor_tensor(q_odd_even, as_parity(G[:, 0:D]), as_parity(vec["bq"][:]),
                                  ALU.add).then_inc(qk_ready, 1)
                dve.tensor_tensor(ksb[:], G[:, D:2 * D], vec["bk"][:], ALU.add).then_inc(qk_ready, 1)

            def qk_stats(t):
                dve.wait_ge(qk_done, t + 1)
                wait(dve, qk_mv, t)
                for a in range(2):
                    dve.bn_stats(qkst[:, a, :], G[:, a * D:(a + 1) * D])
                dve.drain()
                for a in range(2):
                    last = dve.bn_aggr(qkmv[:, a, :], qkst[:, a, :])
                last.then_inc(qk_mv, 1)

            def qk_normalise(t):
                dve.wait_ge(qk_rstd, t + 1)
                wait(dve, qk_ready, 3 * t)
                for a in range(2):
                    dve.tensor_scalar(qkn[:, a, :], G[:, a * D:(a + 1) * D], qkmv[:, a, 0:1], qkrs[:, 1, a:a + 1],
                                      ALU.subtract, ALU.mult).then_inc(qk_norm, 1)

            def v_evacuate(t, p):
                dve.wait_ge(v_done, t + 1)
                wait(dve, av_done, 4 * (t - 1))
                src = G[:, 0:D].rearrange("p (h w) -> p h w", h=H)
                if first:
                    dve.tensor_tensor(vsb[:, p, :, 0:DH], src, vec["bv"][:].rearrange("p (h w) -> p h w", h=H),
                                      ALU.add).then_inc(v_copied, 1)
                else:
                    dve.tensor_copy(vsb[:, p, :, 0:DH], src).then_inc(v_copied, 1)

            def scores_max(t, p):
                dve.wait_ge(s_done, t + 1)
                m = mx[:, p, :]
                wait(dve, pt_done, 4 * (t - 1))
                if first:
                    mrow = mask[:].unsqueeze(1).broadcast_to([P, 4, P])
                    for j in range(NJ):
                        dve.scalar_tensor_tensor(out=SM[:, p, j, :].rearrange("p (h k) -> p h k", h=4),
                                                 in0=Sps[j][:].rearrange("p (h k) -> p h k", h=4),
                                                 scalar=DH ** -0.5, in1=mrow, op0=ALU.mult,
                                                 op1=ALU.add).then_inc(s_copied, 1)
                    dve.wait_ge(s_copied, 4 * (t + 1))
                    wait(dve, shifted, 4 * (t - 1))
                    dve.tensor_reduce(m, SM[:, p, :, :].rearrange("p j (h k) -> p (j h) k", k=P), AX.X,
                                      ALU.max).then_inc(mx_ready, 1)
                else:
                    for j in range(NJ):
                        last = dve.tensor_reduce(m[:, 4 * j:4 * j + 4], Sps[j][:].rearrange("p (h k) -> p h k", h=4),
                                                 AX.X, ALU.max)
                        last.then_inc(mx_ready, 1)
                    for j in range(NJ):
                        dve.wait_ge(mx_ready, 4 * t + j + 1)
                        dve.tensor_tensor(SM[:, p, j, :].rearrange("p (h k) -> p h k", h=4),
                                          Sps[j][:].rearrange("p (h k) -> p h k", h=4),
                                          m[:, 4 * j:4 * j + 4].unsqueeze(2).broadcast_to([P, 4, P]),
                                          ALU.subtract).then_inc(s_copied, 1)

            def divide(t):
                dve.wait_ge(av_done, 4 * (t + 1))
                o = O[:, 0:H * VROW].rearrange("p (h w) -> p h w", h=H)
                dve.reciprocal(rsum[:], o[:, :, DH]).then_inc(rsum_ready, 1)
                dve.wait_ge(rsum_ready, t + 1)
                wait(dve, ot_done, t)
                dve.tensor_tensor(osb[:].rearrange("p (h w) -> p h w", h=H), o[:, :, 0:DH],
                                  rsum[:].unsqueeze(2).broadcast_to([P, H, DH]), ALU.mult).then_inc(o_ready, 1)

            def update(t):
                dve.wait_ge(op_done, t + 1)
                dve.tensor_tensor(delta[:], O[:, 0:D], vec["bo"][:], ALU.add).then_inc(d_ready, 1)
                dve.wait_ge(d_ready, t + 1)
                dve.tensor_tensor(X[:, t, :], X[:, t, :], delta[:], ALU.add).then_inc(x_updated, 1)

            dve.wait_ge(vec_loaded, nvec)
            dve.wait_ge(init, 2)
            if first:
                dve.tensor_scalar(mask[:], mask[:], -1e9, None, ALU.mult).then_inc(init, 1)
                dve.wait_ge(init, 3)
            for t in (0, 1):
                x_stats(t, t)
            for t in (0, 1):
                x_norm(t, t)
            if first:
                qk_evacuate(0)
            else:
                qk_stats(0)
                qk_normalise(0)
            v_evacuate(0, 0)

            def body(i, p):
                if within(i, 0, nt - 2):
                    x_stats(i + 2, p)
                if within(i, 0, nt):
                    scores_max(i, p)
                if within(i, 0, nt - 1):
                    if first:
                        qk_evacuate(i + 1)
                    else:
                        qk_stats(i + 1)
                if within(i, 0, nt - 2):
                    x_norm(i + 2, p)
                if not first and within(i, 0, nt - 1):
                    qk_normalise(i + 1)
                if within(i, 0, nt - 1):
                    v_evacuate(i + 1, 1 - p)
                if within(i, 1, nt + 1):
                    divide(i - 1)
                    update(i - 1)
            over_tiles(dve, nt, body)

        @block.scalar
        def _(act):
            scale = 1.0 if first else D ** -0.5

            def copy(out, in_, done, count, src_free=None):
                act.activation(out, in_, ACT.Copy).then_inc(done, 1)

            def t1(t):
                act.wait_ge(t1_done, t + 1)
                wait(act, v_done, t)
                act.copy(T1s[:].rearrange("p c k -> p (c k)"), G[:]).then_inc(t1_copied, 1)

            def qt(t):
                act.wait_ge(qt_done, t + 1)
                act.copy(qT[:].rearrange("p c k -> p (c k)"), G[:]).then_inc(qt_copied, 1)

            def kt(t):
                act.wait_ge(kt_done, t + 1)
                act.copy(kT[:].rearrange("p c k -> p (c k)"), G[:, 0:D]).then_inc(kt_copied, 1)

            def pt(t):
                for j in range(NJ):
                    act.wait_ge(pt_done, 4 * t + j + 1)
                    wait(act, av_done, 4 * t + j - 1)
                    act.copy(PTs[:, j % 2, :], PTps[j % 2][:]).then_inc(pt_copied, 1)

            def ot(t):
                act.wait_ge(ot_done, t + 1)
                act.copy(oT[:].rearrange("p c k -> p (c k)"), O[:, 0:D]).then_inc(ot_copied, 1)

            def exps(t, p):
                for j in range(NJ):
                    act.wait_ge(shifted if first else s_copied, 4 * t + j + 1)
                    act.activation(SM[:, p, j, :], SM[:, p, j, :], ACT.Exp, scale=scale).then_inc(probs, 1)

            t1(0)
            qt(0)
            kt(0)

            def body(i, p):
                if within(i, 0, nt - 1):
                    t1(i + 1)
                if within(i, 1, nt + 1):
                    pt(i - 1)
                    ot(i - 1)
                if within(i, 0, nt - 1):
                    qt(i + 1)
                    kt(i + 1)
                if within(i, 0, nt):
                    exps(i, p)
            over_tiles(act, nt, body)

        @block.tensor
        def _(pe):
            def t1(t, p, count):
                pe.wait_ge(ctx_loaded[p], count)
                pe.wait_ge(xn_ready, t + 1)
                wait(pe, kt_copied, t)
                for c in range(KC):
                    pe.transpose(G[:, c * P:(c + 1) * P], ctx_sb[:, p, c * P:(c + 1) * P], ident[:])
                for c in range(KC):
                    last = pe.transpose(G[:, (KC + c) * P:(KC + c + 1) * P], xn[:, p, c * P:(c + 1) * P], ident[:])
                last.then_inc(t1_done, 1)

            def product(out, lhs, w):
                for c in range(KC):
                    last = pe.matmul(out, T1s[:, lhs * KC + c, :], w[:, c, :], start=c == 0, stop=c == KC - 1)
                return last

            def qk(t):
                pe.wait_ge(t1_copied, t + 1)
                product(G[:, 0:D], 1, wq)
                product(G[:, D:2 * D], 0, wk).then_inc(qk_done, 1)

            def v(t):
                if first:
                    pe.wait_ge(qk_ready, 2 * (t + 1))
                else:
                    pe.wait_ge(qk_norm, 2 * (t + 1))
                product(G[:, 0:D], 0, wv).then_inc(v_done, 1)

            def q_transpose(t):
                pe.wait_ge(v_copied, t + 1)
                pe.wait_ge(qk_ready, (2 if first else 3) * (t + 1))
                wait(pe, s_done, t)
                for x in range(PAR * KC):
                    last = pe.transpose(G[:, x * P:(x + 1) * P], qpad[:, x * P:(x + 1) * P], ident[:])
                last.then_inc(qt_done, 1)

            def k_transpose(t):
                pe.wait_ge(qt_copied, t + 1)
                for c in range(KC):
                    last = pe.transpose(G[:, c * P:(c + 1) * P], ksb[:, c * P:(c + 1) * P], ident[:])
                last.then_inc(kt_done, 1)

            def scores(t):
                pe.wait_ge(kt_copied, t + 1)
                wait(pe, s_copied, 4 * t)
                for x in range(KC * PAR):
                    c, par = divmod(x, PAR)
                    for j in range(NJ):
                        g = slice(GRP * j, GRP * (j + 1))
                        last = pe.matmul(Sps[j][:, x * P:(x + 1) * P], qT[g, par * KC + c, :], kT[g, c, :],
                                         start=True, stop=True)
                last.then_inc(s_done, 1)

            def weights_transpose(t, p, j):
                pe.wait_ge(probs, 4 * t + j + 1)
                wait(pe, pt_copied, 4 * t + j - 1)
                for x in range(4):
                    last = pe.transpose(PTps[j % 2][:, x * P:(x + 1) * P], SM[:, p, j, x * P:(x + 1) * P], ident[:])
                last.then_inc(pt_done, 1)

            def weigh(t, p, j):
                pe.wait_ge(pt_copied, 4 * t + j + 1)
                for x, (_, _, h) in enumerate(heads_of(j)):
                    last = pe.matmul(O[:, h * VROW:(h + 1) * VROW], PTs[:, j % 2, x * P:(x + 1) * P],
                                     vsb[:, p, h, :], start=True, stop=True)
                last.then_inc(av_done, 1)

            def out_transpose(t):
                pe.wait_ge(o_ready, t + 1)
                for c in range(KC):
                    last = pe.transpose(O[:, c * P:(c + 1) * P], osb[:, c * P:(c + 1) * P], ident[:])
                last.then_inc(ot_done, 1)

            def out_product(t):
                pe.wait_ge(ot_copied, t + 1)
                for c in range(KC):
                    last = pe.matmul(O[:, 0:D], oT[:, c, :], wo[:, c, :], start=c == 0, stop=c == KC - 1)
                last.then_inc(op_done, 1)

            pe.wait_ge(w_loaded, 64)
            t1(0, 0, 16)
            qk(0)
            v(0)
            q_transpose(0)
            k_transpose(0)

            def body(i, p):
                if within(i, 0, nt):
                    scores(i)
                if within(i, 0, nt - 1):
                    t1(i + 1, 1 - p, (8 * i + (8 if p else 0) + 16))
                    qk(i + 1)
                if within(i, 1, nt + 1):
                    wait(pe, x_updated, i - 1)
                    q = 1 - p
                    weights_transpose(i - 1, q, 0)
                    weights_transpose(i - 1, q, 1)
                    weigh(i - 1, q, 0)
                    weights_transpose(i - 1, q, 2)
                    weigh(i - 1, q, 1)
                    weights_transpose(i - 1, q, 3)
                    weigh(i - 1, q, 2)
                    weigh(i - 1, q, 3)
                if within(i, 0, nt - 1):
                    v(i + 1)
                if within(i, 1, nt + 1):
                    out_transpose(i - 1)
                if within(i, 0, nt - 1):
                    q_transpose(i + 1)
                if within(i, 1, nt + 1):
                    out_product(i - 1)
                if within(i, 0, nt - 1):
                    k_transpose(i + 1)
            over_tiles(pe, nt, body)


class Moe:

    def __init__(self, layer, nt, io):
        self.layer, self.nt = layer, nt
        names = ("L0_ffn_w1", "L0_ffn_w3", "L0_ffn_w2") if layer == 0 else ("L1_ffn_Wg", "L1_ffn_Wu", "L1_ffn_Wd")
        self.gate, self.up, self.down = (io[n] for n in names)
        self.E, _, self.F = self.gate.shape
        self.units = self.F // BANK
        self.tiles = (2 * nt * P + self.E * (P - 1)) // P
        self.router = io["L0_ffn_router_w"] if layer == 0 else io["L1_ffn_gate_w"]


def load_experts(core, moe, eng):
    g, u, d = core.expert_views(moe)
    eng.dma_start(g, moe.gate.rearrange("e (c p) f -> p e c f", p=P)).then_inc(core.experts_loaded, 16)
    eng.dma_start(u, moe.up.rearrange("e (c p) f -> p e c f", p=P)).then_inc(core.experts_loaded, 16)
    eng.dma_start(d, moe.down.rearrange("e (c p) f -> p e c f", p=P)).then_inc(core.experts_loaded, 16)


def router(core, io, moe, st):
    nc = core.nc
    nt, E, S = moe.nt, moe.E, moe.tiles
    second = moe.layer == 1
    N = f"r{moe.layer}_"
    X, Xn, ident = core.X, st["Xn"], core.ident
    with ExitStack() as ctx:
        sem = core.phase_sems(ctx, N)
        sb = lambda name, shape, dt=F32: core.sb(N + name, shape, ctx, dt)
        rw = sb("rw", [P, KC, E])
        upper, ones = sb("upper", [P, P]), sb("ones", [P, P])
        st1, mv1, rs1 = sb("st1", [P, nt, 6]), st["mean_var"], st["rstd"]
        var = sb("var", [P, nt])
        xr = sb("xr", [P, 2, D])
        xrT = sb("xrT", [P, KC, P])
        ints = sb("ints", [P, 256], mybir.dt.int32)
        idx_rev, tile_no, tok_no = sb("idx_rev", [P, E]), sb("tile_no", [P, S]), sb("tok_no", [P, nt])
        big = [sb(f"big{i}", [P, nt, E]) for i in range(9)]
        LG, PR, oh1, oh2, tmp, M, A, B, TOT = big
        small = [sb(f"small{i}", [P, nt]) for i in range(9)]
        mx, sm, m1, m2, c1, den, rden, s1, s2 = small
        cmp_cnt, cnt_t, end_a, end_b, start = sb("cmp_cnt", [P, E, nt]), sb("cnt_t", [P, E]), sb("end_a", [P, E]), sb("end_b", [P, E]), sb("start", [P, E])
        cmp_tile, eid_f = sb("cmp_tile", [P, S, E - 1]), sb("eid_f", [P, S])
        if second:
            st2, mv2, rs2 = sb("st2", [P, nt, 6]), sb("mv2", [P, nt, 2]), sb("rs2", [P, nt])
            ln_s, ln_b = sb("ln_s", [P, D]), sb("ln_b", [P, D])
            xq = sb("xq", [P, 2, D])
        else:
            rb = sb("rb", [P, E])
        Tb, LB, PREb, TOTb = core.bank[0], core.bank[1], core.bank[2], core.bank[3]

        w_loaded, consts, stats, rstd, normed = sem("w_loaded"), sem("consts"), sem("stats"), sem("rstd"), sem("normed")
        xr_ready, t_done, t_copied, lg_done = sem("xr_ready"), sem("t_done"), sem("t_copied"), sem("lg_done")
        to_exp, expd, counted, prefix, chain = sem("to_exp"), sem("expd"), sem("counted"), sem("prefix"), sem("chain")
        pool_chain = sem("pool_chain")
        if second:
            xq_ready, scaled = sem("xq_ready"), sem("scaled")

        nload = 48 if second else 32
        block = ctx.enter_context(nc.Block())

        @block.sync
        def _(sp):
            sp.dma_start(rw[:], moe.router.rearrange("(c p) e -> p c e", p=P)).then_inc(w_loaded, 16)
            if second:
                sp.dma_start(ln_s[:], io["L1_ffn_ln_scale"].partition_broadcast(P)).then_inc(w_loaded, 16)
                sp.dma_start(ln_b[:], io["L1_ffn_ln_bias"].partition_broadcast(P)).then_inc(w_loaded, 16)
            else:
                sp.dma_start(rb[:], io["L0_ffn_router_b"].partition_broadcast(P)).then_inc(w_loaded, 16)

        @block.gpsimd
        def _(pool):
            made = [0]

            def link(ins):
                made[0] += 1
                ins.then_inc(pool_chain, 1)
                pool.wait_ge(pool_chain, made[0])

            link(pool.memset(upper[:], 1.0))
            pool.affine_select(out=upper[:], in_=upper[:], compare_op=ALU.is_gt, fill=0.0, base=0,
                               pattern=[[1, P]], channel_multiplier=-1).then_inc(consts, 1)
            pool.memset(ones[:], 1.0).then_inc(consts, 1)
            link(pool.iota(ints[:, 0:E], pattern=[[-1, E]], base=E, channel_multiplier=0))
            pool.tensor_copy(idx_rev[:], ints[:, 0:E]).then_inc(consts, 1)
            link(pool.iota(ints[:, E:E + S], pattern=[[1, S]], base=0, channel_multiplier=0))
            pool.tensor_copy(tile_no[:], ints[:, E:E + S]).then_inc(consts, 1)
            link(pool.iota(ints[:, E + S:E + S + nt], pattern=[[P, nt]], base=0, channel_multiplier=0))
            pool.tensor_copy(tok_no[:], ints[:, E + S:E + S + nt]).then_inc(consts, 1)

            def std(mv, out, turn):
                pool.wait_ge(stats, turn)
                link(pool.tensor_tensor(var[:], mv[:, :, 1], core.eps[:].broadcast_to([P, nt]), ALU.add))
                pool.tensor_tensor(out[:], var[:], core.minus_half[:], ALU.pow).then_inc(rstd, 1)
            std(mv1, rs1, 1)
            if second:
                pool.wait_ge(rstd, 1)
                std(mv2, rs2, 2)
                pool.wait_ge(w_loaded, nload)

                def body(t, p):
                    if within(t, 0, nt):
                        pool.wait_ge(xq_ready, t + 1)
                        pool.tensor_tensor(xq[:, p, :], xq[:, p, :], ln_s[:], ALU.mult).then_inc(scaled, 1)
                        wait(pool, t_done, t - 1)
                        pool.wait_ge(scaled, t + 1)
                        pool.tensor_tensor(xr[:, p, :], xq[:, p, :], ln_b[:], ALU.add).then_inc(xr_ready, 1)
                over_tiles(pool, nt, body)

        @block.tensor
        def _(pe):
            pe.wait_ge(w_loaded, nload)

            def body(t, p):
                if not within(t, 0, nt):
                    return
                pe.wait_ge(xr_ready, t + 1)
                wait(pe, t_copied, t)
                for c in range(KC):
                    last = pe.transpose(Tb[:, c * P:(c + 1) * P], xr[:, p, c * P:(c + 1) * P], ident[:])
                last.then_inc(t_done, 1)
                pe.wait_ge(t_copied, t + 1)
                for c in range(KC):
                    last = pe.matmul(LB[:, bass.ds(t * E, E)], xrT[:, c, :], rw[:, c, :], start=c == 0, stop=c == KC - 1)
                last.then_inc(lg_done, 1)
            over_tiles(pe, nt, body)
            pe.wait_ge(consts, 5)
            pe.wait_ge(counted, 1)
            flat = M[:].rearrange("p t e -> p (t e)")
            pe.matmul(PREb[:, 0:nt * E], upper[:], flat, start=True, stop=True)
            pe.matmul(TOTb[:, 0:nt * E], ones[:], flat, start=True, stop=True).then_inc(prefix, 1)

        @block.scalar
        def _(act):
            def body(t, p):
                if within(t, 0, nt):
                    act.wait_ge(t_done, t + 1)
                    wait(act, lg_done, t)
                    act.copy(xrT[:].rearrange("p c k -> p (c k)"), Tb[:, 0:D]).then_inc(t_copied, 1)
            over_tiles(act, nt, body)
            act.wait_ge(to_exp, 1)
            act.activation(PR[:], LG[:], ACT.Exp).then_inc(expd, 1)

        @block.vector
        def _(dve):
            made = [0]

            def link(ins):
                made[0] += 1
                ins.then_inc(chain, 1)
                dve.wait_ge(chain, made[0])

            def stats_of(src, stx, mv):
                with dve.Fori(0, nt) as t:
                    dve.bn_stats(stx[:, t, :], src[:, t, :])
                dve.drain()
                for t in range(nt):
                    last = dve.bn_aggr(mv[:, t, :], stx[:, t, :])
                last.then_inc(stats, 1)

            stats_of(X, st1, mv1)
            dve.wait_ge(rstd, 1)
            with dve.Fori(0, nt) as t:
                dve.tensor_scalar(Xn[:, t, :], X[:, t, :], mv1[:, t, 0:1], rs1[:, bass.ds(t, 1)],
                                  ALU.subtract, ALU.mult).then_inc(normed, 1)
            if second:
                dve.wait_ge(normed, nt)
                stats_of(Xn, st2, mv2)
                dve.wait_ge(rstd, 2)

                def body(t, p):
                    if within(t, 0, nt):
                        wait(dve, scaled, t - 1)
                        wait(dve, xr_ready, t - 1)
                        dve.tensor_scalar(xq[:, p, :], Xn[:, t, :], mv2[:, t, 0:1], rs2[:, bass.ds(t, 1)],
                                          ALU.subtract, ALU.mult).then_inc(xq_ready, 1)
            else:
                def body(t, p):
                    if within(t, 0, nt):
                        wait(dve, t_done, t - 1)
                        dve.tensor_scalar(xr[:, p, :], X[:, t, :], mv1[:, t, 0:1], rs1[:, bass.ds(t, 1)],
                                          ALU.subtract, ALU.mult).then_inc(xr_ready, 1)
            over_tiles(dve, nt, body)

            tt, red = dve.tensor_tensor, dve.tensor_reduce
            shape = [P, nt, E]
            along = lambda a: a[:].unsqueeze(2).broadcast_to(shape)
            idx = idx_rev[:].unsqueeze(1).broadcast_to(shape)
            logits = LB[:, 0:nt * E].rearrange("p (t e) -> p t e", e=E)
            dve.wait_ge(lg_done, nt)
            dve.wait_ge(w_loaded, nload)
            dve.wait_ge(consts, 5)
            if second:
                link(dve.tensor_copy(LG[:], logits))
            else:
                link(tt(LG[:], logits, rb[:].unsqueeze(1).broadcast_to(shape), ALU.add))
            link(red(mx[:], LG[:], AX.X, ALU.max))
            tt(LG[:], LG[:], along(mx), ALU.subtract).then_inc(to_exp, 1)
            dve.wait_ge(expd, 1)
            link(red(sm[:], PR[:], AX.X, ALU.add))
            link(dve.reciprocal(rden[:], sm[:]))
            link(tt(PR[:], PR[:], along(rden), ALU.mult))
            link(red(m1[:], PR[:], AX.X, ALU.max))
            link(tt(tmp[:], PR[:], along(m1), ALU.is_equal))
            link(tt(tmp[:], tmp[:], idx, ALU.mult))
            link(red(c1[:], tmp[:], AX.X, ALU.max))
            link(tt(oh1[:], along(c1), idx, ALU.is_equal))
            link(dve.scalar_tensor_tensor(out=M[:], in0=oh1[:], scalar=-2.0, in1=PR[:], op0=ALU.mult, op1=ALU.add))
            link(red(m2[:], M[:], AX.X, ALU.max))
            link(tt(tmp[:], M[:], along(m2), ALU.is_equal))
            link(tt(tmp[:], tmp[:], idx, ALU.mult))
            link(red(c1[:], tmp[:], AX.X, ALU.max))
            link(tt(oh2[:], along(c1), idx, ALU.is_equal))
            tt(M[:], oh1[:], oh2[:], ALU.add).then_inc(counted, 1)
            link(tt(den[:], m1[:], m2[:], ALU.add))
            if second:
                link(dve.tensor_scalar(den[:], den[:], EPS, None, ALU.add))
            link(dve.reciprocal(rden[:], den[:]))
            link(tt(st["gate"][:, 0, :], m1[:], rden[:], ALU.mult))
            link(tt(st["gate"][:, 1, :], m2[:], rden[:], ALU.mult))
            dve.wait_ge(prefix, 1)
            link(dve.tensor_copy(TOT[:], TOTb[:, 0:nt * E].rearrange("p (t e) -> p t e", e=E)))
            src, dst, step = TOT, A, 1
            while step < nt:
                link(tt(dst[:, step:, :], src[:, step:, :], src[:, 0:nt - step, :], ALU.add))
                link(dve.tensor_copy(dst[:, 0:step, :], src[:, 0:step, :]))
                src, dst, step = dst, (B if dst is A else A), step * 2
            total = src
            cnt = total[:, nt - 1, :].unsqueeze(2).broadcast_to([P, E, nt])
            link(tt(cmp_cnt[:], cnt, tok_no[:].unsqueeze(1).broadcast_to([P, E, nt]), ALU.is_gt))
            link(red(cnt_t[:], cmp_cnt[:], AX.X, ALU.add))
            a, b, step = cnt_t, end_a, 1
            while step < E:
                link(tt(b[:, step:], a[:, step:], a[:, 0:E - step], ALU.add))
                link(dve.tensor_copy(b[:, 0:step], a[:, 0:step]))
                a, b, step = b, (end_b if b is end_a else end_a), step * 2
            end = a
            link(tt(cmp_tile[:], tile_no[:].unsqueeze(2).broadcast_to([P, S, E - 1]),
                    end[:, 0:E - 1].unsqueeze(1).broadcast_to([P, S, E - 1]), ALU.is_ge))
            link(red(eid_f[:], cmp_tile[:], AX.X, ALU.add))
            link(dve.tensor_copy(st["expert"][:], eid_f[:]))
            link(tt(start[:], end[:], cnt_t[:], ALU.subtract))
            link(dve.tensor_scalar(start[:], start[:], float(P), None, ALU.mult))
            link(tt(tmp[:], total[:], TOT[:], ALU.subtract))
            link(tt(tmp[:], tmp[:], start[:].unsqueeze(1).broadcast_to(shape), ALU.add))
            link(tt(tmp[:], PREb[:, 0:nt * E].rearrange("p (t e) -> p t e", e=E), tmp[:], ALU.add))
            for which, oh in enumerate((oh1, oh2)):
                link(tt(M[:], tmp[:], oh[:], ALU.mult))
                link(red((s1, s2)[which][:], M[:], AX.X, ALU.add))
                link(dve.tensor_copy(st["slot"][:, which, :], (s1, s2)[which][:]))


def scatter(core, moe, st, pool, done):
    pool.wait_ge(st["zeroed"], 16)
    for t in range(moe.nt):
        for which in range(2):
            pool.indirect_dma_start(out=st["xs"], out_offset=bass.IndirectOffsetOnAxis(
                ap=st["slot"][:, which, t:t + 1], axis=0), in_=st["Xn"][:, t, :], in_offset=None).then_inc(done, 16)
    pool.wait_ge(done, 16 * 2 * moe.nt)


def ffn(core, io, moe, st, routed):
    nc = core.nc
    n = moe.tiles if routed else moe.nt
    U = moe.units
    N = f"f{moe.layer}{'r' if routed else 's'}_"
    X, ident = core.X, core.ident
    with ExitStack() as ctx:
        sem = core.phase_sems(ctx, N)
        sb = lambda name, shape: core.sb(N + name, shape, ctx)
        xin, xT = sb("xin", [P, 2, D]), sb("xT", [P, 2, KC, P])
        sg, hid, hidT = sb("sg", [P, 2, BANK]), sb("hid", [P, 2, BANK]), sb("hidT", [P, 2, BANK])
        y = sb("y", [P, 2, D])
        if not routed:
            wg, wu = sb("wg", [P, KC, moe.F]), sb("wu", [P, KC, moe.F])
            wd = sb("wd", [P, moe.F // P, D])

        def ring(p, u):
            return u if U == 2 else p

        Gb, Ub, HTb = core.bank[0:2], core.bank[2:4], core.bank[4:6]
        Yb, XTb = core.bank[6], core.bank[7]

        x_in = [sem("x_in0"), sem("x_in1")]
        w_loaded, x_ready, xt_done, xt_copied = sem("w_loaded"), sem("x_ready"), sem("xt_done"), sem("xt_copied")
        g_done, u_done, silu_done, hid_ready, ht_done, ht_copied, half_done = (
            sem(s) for s in ("g_done", "u_done", "silu_done", "hid_ready", "ht_done", "ht_copied", "half_done"))
        y_done, y_copied, stored, scattered = sem("y_done"), sem("y_copied"), sem("stored"), sem("scattered")
        stored = [sem("stored0"), sem("stored1")]

        block = ctx.enter_context(nc.Block())

        @block.sync
        def _(sp):
            if not routed:
                for dst, name in ((wg, "sWg"), (wu, "sWu"), (wd, "sWd")):
                    sp.dma_start(dst[:], io[f"L1_ffn_{name}"].rearrange("(c p) f -> p c f", p=P)).then_inc(w_loaded, 16)
                return

            def body(i, p):
                if within(i, 0, n):
                    wait(sp, xt_done, i - 1)
                    sp.dma_start(xin[:, p, :], st["xs"][bass.ds(i * P, P), :]).then_inc(x_in[p], 16)
            over_tiles(sp, n, body)
            sp.wait_ge(stored[0], 16 * ((n + 1) // 2))
            sp.wait_ge(stored[1], 16 * (n // 2))

        if not routed:
            @block.gpsimd
            def _(pool):
                scatter(core, moe, st, pool, scattered)

        @block.tensor
        def _(pe):
            pe.wait_ge(core.experts_loaded, 48 * (moe.layer + 1))
            if not routed:
                pe.wait_ge(w_loaded, 48)

            def weights(i):
                if not routed:
                    return wg, wu, wd
                e = pe.value_load(st["expert"][0:1, bass.ds(i, 1)], min_val=0, max_val=moe.E - 1)
                return tuple(v[:, bass.ds(e, 1)].squeeze(1) for v in core.expert_views(moe))

            def x_transpose(i, p, count):
                if routed:
                    pe.wait_ge(x_in[p], count)
                else:
                    pe.wait_ge(x_ready, i + 1)
                wait(pe, xt_copied, i)
                for c in range(KC):
                    last = pe.transpose(XTb[:, c * P:(c + 1) * P], xin[:, p, c * P:(c + 1) * P], ident[:])
                last.then_inc(xt_done, 1)

            def product(bank, i, p, u, w):
                for c in range(KC):
                    last = pe.matmul(bank[:], xT[:, p, c, :], w[:, c, u * BANK:(u + 1) * BANK],
                                     start=c == 0, stop=c == KC - 1)
                return last

            def gate(i, p, u, w):
                k, r = i * U + u, ring(p, u)
                pe.wait_ge(xt_copied, i + 1)
                wait(pe, silu_done, k - 1)
                product(Gb[r], i, p, u, w[0]).then_inc(g_done, 1)

            def up(i, p, u, w):
                k, r = i * U + u, ring(p, u)
                wait(pe, hid_ready, k - 1)
                product(Ub[r], i, p, u, w[1]).then_inc(u_done, 1)

            def hid_transpose(i, p, u):
                k, r = i * U + u, ring(p, u)
                pe.wait_ge(hid_ready, k + 1)
                wait(pe, ht_copied, k - 1)
                for c in range(4):
                    last = pe.transpose(HTb[r][:, c * P:(c + 1) * P], hid[:, r, c * P:(c + 1) * P], ident[:])
                last.then_inc(ht_done, 1)

            def down(i, p, u, w):
                k, r = i * U + u, ring(p, u)
                pe.wait_ge(ht_copied, k + 1)
                if u == 0:
                    wait(pe, y_copied, i)
                for c in range(4):
                    last = pe.matmul(Yb[:, 0:D], hidT[:, r, c * P:(c + 1) * P], w[2][:, u * 4 + c, :],
                                     start=u == 0 and c == 0, stop=u == U - 1 and c == 3)
                last.then_inc(y_done if u == U - 1 else half_done, 1)

            x_transpose(0, 0, 16)

            def body(i, p):
                w_now = weights(i) if within(i, 0, n) else None
                for u in range(U):
                    prev = (i, p, u - 1) if u else (i - 1, 1 - p, U - 1)
                    there = within(i, 0, n) if u else within(i, 1, n + 1)
                    if within(i, 0, n):
                        gate(i, p, u, w_now)
                    if there:
                        hid_transpose(*prev)
                    if u == 0 and within(i, 0, n - 1):
                        x_transpose(i + 1, 1 - p, 8 * i + 8 * p + 16)
                    if within(i, 0, n):
                        up(i, p, u, w_now)
                    if there:
                        down(*prev, w_now if u else weights(i - 1))
            over_tiles(pe, n, body)

        @block.scalar
        def _(act):
            def xt(i, p):
                act.wait_ge(xt_done, i + 1)
                wait(act, u_done, (i - 1) * U)
                act.copy(xT[:, p].rearrange("p c k -> p (c k)"), XTb[:, 0:D]).then_inc(xt_copied, 1)

            def silu(i, p, u):
                k, r = i * U + u, ring(p, u)
                act.wait_ge(g_done, k + 1)
                wait(act, hid_ready, k - 1)
                act.activation(sg[:, r, :], Gb[r][:], ACT.Silu).then_inc(silu_done, 1)

            def ht(i, p, u):
                k, r = i * U + u, ring(p, u)
                act.wait_ge(ht_done, k + 1)
                act.copy(hidT[:, r, :], HTb[r][:]).then_inc(ht_copied, 1)

            def leave(i, p):
                act.wait_ge(y_copied, i + 1)
                act.dma_start(st["ys"][bass.ds(i * P, P), :], y[:, p, :]).then_inc(stored[p], 16)

            xt(0, 0)

            def body(i, p):
                for u in range(U):
                    if within(i, 0, n):
                        silu(i, p, u)
                    if routed and u == 0 and within(i, 2, n + 2):
                        leave(i - 2, p)
                    if u == 0:
                        if within(i, 1, n + 1):
                            ht(i - 1, 1 - p, U - 1)
                        if within(i, 0, n - 1):
                            xt(i + 1, 1 - p)
                    elif within(i, 0, n):
                        ht(i, p, u - 1)
            over_tiles(act, n, body, extra=2)

        @block.vector
        def _(dve):
            def normalise(i, p):
                wait(dve, xt_done, i - 1)
                dve.tensor_scalar(xin[:, p, :], X[:, i, :], st["mean_var"][:, i, 0:1], st["rstd"][:, bass.ds(i, 1)],
                                  ALU.subtract, ALU.mult).then_inc(x_ready, 1)

            def multiply(i, p, u):
                k, r = i * U + u, ring(p, u)
                dve.wait_ge(silu_done, k + 1)
                dve.wait_ge(u_done, k + 1)
                wait(dve, ht_done, k - 1)
                dve.tensor_tensor(hid[:, r, :], Ub[r][:], sg[:, r, :], ALU.mult).then_inc(hid_ready, 1)

            def result(i, p, stores):
                dve.wait_ge(y_done, i + 1)
                if routed:
                    wait(dve, stored[p], stores)
                    dve.tensor_scalar(y[:, p, :], Yb[:, 0:D], 1.0, None, ALU.mult).then_inc(y_copied, 1)
                else:
                    dve.tensor_tensor(X[:, i, :], Yb[:, 0:D], X[:, i, :], ALU.add).then_inc(y_copied, 1)

            if not routed:
                normalise(0, 0)

            def body(i, p):
                if not routed and within(i, 0, n - 1):
                    normalise(i + 1, 1 - p)
                for u in range(U):
                    if within(i, 0, n):
                        multiply(i, p, u)
                    if u == 0 and within(i, 1, n + 1):
                        result(i - 1, 1 - p, 8 * (i - 2 + p))
            over_tiles(dve, n, body)


def dispatch(core, moe, st):
    done = core.sem(f"d{moe.layer}_scattered")
    with core.nc.Block() as block:

        @block.gpsimd
        def _(pool):
            scatter(core, moe, st, pool, done)


def combine(core, moe, st):
    nc, nt, X = core.nc, moe.nt, core.X
    N = f"c{moe.layer}_"
    R = 4
    with ExitStack() as ctx:
        sem = core.phase_sems(ctx, N)
        rows = core.sb(N + "rows", [P, R, 2, D], ctx)
        got = [sem(f"gathered{r}") for r in range(R)]
        added, half = sem("added"), sem("half")
        block = ctx.enter_context(nc.Block())

        @block.gpsimd
        def _(pool):
            for t in range(nt):
                wait(pool, added, t - R + 1)
                for which in range(2):
                    pool.indirect_dma_start(out=rows[:, t % R, which, :], out_offset=None, in_=st["ys"],
                                            in_offset=bass.IndirectOffsetOnAxis(
                                                ap=st["slot"][:, which, t:t + 1], axis=0)).then_inc(got[t % R], 16)

        @block.vector
        def _(dve):
            with dve.Fori(0, nt // R) as turn:
                for r in range(R):
                    t = turn * R + r
                    dve.wait_ge(got[r], 32 * (turn + 1))
                    dve.scalar_tensor_tensor(out=X[:, t, :], in0=rows[:, r, 0, :], scalar=st["gate"][:, 0, bass.ds(t, 1)],
                                             in1=X[:, t, :], op0=ALU.mult, op1=ALU.add).then_inc(half, 1)
                    dve.wait_ge(half, t + 1)
                    dve.scalar_tensor_tensor(out=X[:, t, :], in0=rows[:, r, 1, :], scalar=st["gate"][:, 1, bass.ds(t, 1)],
                                             in1=X[:, t, :], op0=ALU.mult, op1=ALU.add).then_inc(added, 1)


def experts(core, io, moe):
    with ExitStack() as ctx:
        sb = lambda name, shape, dt=F32: core.sb(f"m{moe.layer}_{name}", shape, ctx, dt)
        S = moe.tiles
        st = {
            "mean_var": sb("mean_var", [P, moe.nt, 2]), "rstd": sb("rstd", [P, moe.nt]),
            "gate": sb("gate", [P, 2, moe.nt]), "slot": sb("slot", [P, 2, moe.nt], mybir.dt.int32),
            "expert": sb("expert", [P, S], mybir.dt.int32),
            "xs": core.slots_in[moe.layer], "ys": core.slots_out[moe.layer], "zeroed": core.zeroed[moe.layer],
        }
        with ExitStack() as inner:
            st["Xn"] = core.sb(f"m{moe.layer}_Xn", [P, moe.nt, D], inner)
            router(core, io, moe, st)
            if moe.layer == 0:
                dispatch(core, moe, st)
            else:
                ffn(core, io, moe, st, routed=False)
        ffn(core, io, moe, st, routed=True)
        combine(core, moe, st)


def store(core, io, out):
    done = core.sem("stored")
    with core.nc.Block() as block:

        @block.sync
        def _(sp):
            nt = core.X.shape[1]
            for c in range(4):
                part = slice(c * nt // 4, (c + 1) * nt // 4)
                sp.dma_start(out[part].rearrange("t p d -> p t d"), core.X[:, part, :]).then_inc(done, 16)
            sp.wait_ge(done, 64)


STAGES = 4


def build(nc, io, out):
    nt = io["x"].shape[0]
    with ExitStack() as stack:
        core = Core(nc, stack)
        core.X = core.sb("X", [P, nt, D])
        core.ident = core.sb("ident", [P, P])
        core.minus_half = core.sb("minus_half", [P, nt])
        core.eps = core.sb("eps", [P, 1])
        core.zeros = core.sb("zeros", [P, D])
        moes = [Moe(layer, nt, io) for layer in range(2)]
        size = max(m.E * m.F * KC for m in moes)
        core.W = core.sb("W", [P, 3, size])
        core.slots_in = [nc.dram_tensor(f"slots_in{m.layer}", (m.tiles * P, D), F32).ap() for m in moes]
        core.slots_out = [nc.dram_tensor(f"slots_out{m.layer}", (m.tiles * P, D), F32).ap() for m in moes]
        core.zeroed = [core.sem(f"slots_zeroed{m.layer}") for m in moes]
        core.x_loaded = core.sem("x_loaded")
        core.experts_loaded = core.sem("experts_loaded")
        core.bank = [stack.enter_context(nc.psum_tensor(f"bank{b}", [P, BANK], F32)) for b in range(8)]
        load_constants(core, io)
        attention(core, io, 0, nt, moes[0])
        if STAGES >= 2:
            experts(core, io, moes[0])
        if STAGES >= 3:
            attention(core, io, 1, nt, moes[1])
        if STAGES >= 4:
            experts(core, io, moes[1])
        store(core, io, out)


def kernel(**inputs):
    import numpy as np
    import concourse.bacc as bacc
    from concourse.bass_utils import run_bass_kernel_spmd

    nc = bacc.Bacc("TRN2", target_bir_lowering=False, num_devices=1)
    arrays, io = {}, {}
    for name, value in inputs.items():
        a = np.ascontiguousarray(np.asarray(value).T if name == "L1_ffn_gate_w" else np.asarray(value))
        arrays[name] = a
        io[name] = nc.dram_tensor(name, a.shape, mybir.dt.from_np(a.dtype), kind="ExternalInput").ap()
    out = nc.dram_tensor("out", inputs["x"].shape, F32, kind="ExternalOutput").ap()
    build(nc, io, out)
    result = run_bass_kernel_spmd(nc, [arrays], core_ids=[0])
    return result.results[0]["out"]
```

```python
from contextlib import ExitStack

import concourse.bass as bass
from concourse import mybir

F32 = mybir.dt.float32
ALU = mybir.AluOpType
ACT = mybir.ActivationFunctionType
AX = mybir.AxisListType

P = 128
D = 256
KC = D // P
H = 16
DH = D // H
EPS = 1e-5
GRP = 32
PAR = 2
NJ = P // GRP
QROW = D + DH
VROW = DH + 1
BANK = 512
ROW = D + 2


def wait(eng, sem, value):
    if isinstance(value, int) and value <= 0:
        return
    eng.wait_ge(sem, value)


def over_tiles(eng, n, body, extra=1):
    first, turns = 4, n // 2 - 1
    for i in range(first):
        body(i, i % 2)
    with eng.Fori(first // 2, turns) as turn:
        for p in (0, 1):
            body(2 * turn + p, p)
    for i in range(2 * turns, n + extra):
        body(i, i % 2)


def within(i, low, high):
    return not isinstance(i, int) or low <= i < high


class Core:

    def __init__(self, nc, stack):
        self.nc, self.stack = nc, stack

    def expert_views(self, moe):
        n = moe.E * moe.F * KC
        g, u = (self.W[:, a, 0:n].rearrange("p (e c f) -> p e c f", e=moe.E, c=KC) for a in (0, 1))
        return g, u, self.W[:, 2, 0:n].rearrange("p (e c d) -> p e c d", e=moe.E, d=D)

    def results_of(self, layer):
        rows = 2 * self.X.shape[1] * P
        return self.results[layer][1:1 + rows, :].rearrange("(w t p) d -> t p w d", w=2, p=P)

    def phase_sems(self, ctx, prefix):
        taken = []

        def clear():
            with self.nc.Block() as block:

                @block.gpsimd
                def _(pool):
                    for s in taken:
                        pool.sem_clear(s)

        def sem(name):
            taken.append(sems.enter_context(self.nc.semaphore(prefix + name)))
            return taken[-1]

        sems = ctx.enter_context(ExitStack())
        ctx.callback(clear)
        return sem

    def sem(self, name):
        return self.stack.enter_context(self.nc.semaphore(name))

    def sb(self, name, shape, stack=None, dt=F32):
        return (stack or self.stack).enter_context(self.nc.sbuf_tensor(name, shape, dt))


def load_x(core, io, eng, c):
    n = core.X.shape[1] // 4
    part = slice(c * n, (c + 1) * n)
    eng.dma_start(core.X[:, part, :], io["x"][part].rearrange("t p d -> p t d")).then_inc(core.x_loaded[min(c, 1)], 16)


def load_constants(core, io):
    nc = core.nc
    zeroed, ready = core.sem("ident_zeroed"), core.sem("constants_ready")
    with nc.Block() as block:

        @block.sync
        def _(sp):
            load_x(core, io, sp, 0)

        @block.gpsimd
        def _(pool):
            pool.memset(core.ident[:], 0.0).then_inc(zeroed, 1)
            pool.wait_ge(zeroed, 1)
            pool.affine_select(out=core.ident[:], in_=core.ident[:], compare_op=ALU.not_equal, fill=1.0,
                               base=0, pattern=[[-1, P]], channel_multiplier=1).then_inc(ready, 1)
            pool.memset(core.minus_half[:], -0.5).then_inc(ready, 1)
            pool.memset(core.eps[:], EPS).then_inc(ready, 1)
            pool.memset(core.zeros[:], 0.0).then_inc(ready, 1)
            pool.wait_ge(ready, 4)


def attention(core, io, layer, nt, moe, st):
    E = moe.E
    nc = core.nc
    first = layer == 0
    N = f"a{layer}_"
    X, ident = core.X, core.ident
    with ExitStack() as ctx:
        sem = core.phase_sems(ctx, N)
        sb = lambda name, shape: core.sb(N + name, shape, ctx)
        wq, wk, wv, wo = (sb(w, [P, KC, D]) for w in ("wq", "wk", "wv", "wo"))
        rows = ["bq", "bk", "bv", "bo"] if first else ["bo", "q_gamma", "q_beta", "k_gamma", "k_beta"]
        vec = {r: sb(r, [P, D]) for r in rows}
        ctx_sb = sb("ctx", [P, 2, D])
        xn = sb("xn", [P, 2, D])
        T1s = sb("ctxT_xnT", [P, 2, 4, P])
        qpad = sb("qpad", [P, PAR * QROW])
        ksb = sb("ksb", [P, D])
        vsb = sb("vsb", [P, 2, H, VROW])
        qT = sb("qT", [P, PAR * KC, P])
        kT = sb("kT", [P, KC, NJ, P])
        xrT = sb("routerT", [P, KC, P])
        SM = sb("scores", [P, 2, NJ, BANK])
        mx = sb("mx", [P, 2, H])
        PTs = sb("weightsT", [P, 2, BANK])
        rsum = sb("rsum", [P, H])
        osb = sb("osb", [P, D])
        oT = sb("oT", [P, KC, P])
        delta = sb("delta", [P, D])
        xst, xmv, xrs = sb("xst", [P, 2, 6]), sb("xmv", [P, 2, 2]), sb("xrs", [P, 2, 2])
        nst, nmv, nrs = sb("nst", [P, 2, 6]), sb("nmv", [P, 2, 3]), sb("nrs", [P, 2])
        xr = sb("xr", [P, 2, D])
        rw = sb("rw", [P, KC, E])
        if first:
            mask = sb("mask", [P, P])
            rb = sb("rb", [P, E])
            before = None
        else:
            before = core.results_of(0)
            zin = sb("zin", [P, 2, 2, D])
            z_loaded, z_added = [sem("z_loaded0"), sem("z_loaded1")], sem("z_added")
        if not first:
            xn2, rst, rmv, rrs = sb("xn2", [P, 2, D]), sb("rst", [P, 2, 6]), sb("rmv", [P, 2, 2]), sb("rrs", [P, 2, 2])
            ln_s, ln_b = sb("ln_s", [P, D]), sb("ln_b", [P, D])
            qkst, qkmv, qkrs = sb("qkst", [P, 2, 6]), sb("qkmv", [P, 2, 2]), sb("qkrs", [P, 2, 2])
            qkn = sb("qkn", [P, 2, D])

        Sps = [core.bank[j] for j in range(NJ)]
        PTps = [core.bank[4], core.bank[5]]
        G, O = core.bank[6], core.bank[7]
        T1ps = core.bank[0]

        def heads_of(b):
            c, par = divmod(b, PAR)
            return [(c * NJ + j) * PAR + par for j in range(NJ)]

        q_odd_even = qpad[:].rearrange("p (r w) -> p r w", r=PAR)[:, :, 0:D].rearrange(
            "p r (m w) -> p r m w", w=PAR * DH)[:, :, :, 0:DH]

        def as_parity(ap):
            return ap.rearrange("p (m r w) -> p r m w", r=PAR, w=DH)

        w_loaded, vec_loaded, init = sem("w_loaded"), sem("vec_loaded"), sem("buffers_set")
        ctx_loaded = [sem("ctx_loaded0"), sem("ctx_loaded1")]
        x_mv, x_var, x_rstd, xn_ready = (sem(s) for s in ("x_mv", "x_var", "x_rstd", "xn_ready"))
        t1_done, t1_copied = sem("t1_done"), sem("t1_copied")
        qk_done, qk_copied, qk_ready = sem("qk_done"), sem("qk_copied"), sem("qk_ready")
        v_done, v_copied = sem("v_done"), sem("v_copied")
        qt_done, qt_copied, kt_done, kt_copied = (sem(s) for s in ("qt_done", "qt_copied", "kt_done", "kt_copied"))
        s_done, s_copied, mx_ready, shifted, probs = (sem(s) for s in ("s_done", "s_copied", "mx_ready", "shifted", "probs"))
        pt_done, pt_copied, av_done = sem("pt_done"), sem("pt_copied"), sem("av_done")
        rsum_ready, o_ready, ot_done, ot_copied = (sem(s) for s in ("rsum_ready", "o_ready", "ot_done", "ot_copied"))
        op_done, d_ready, x_updated = sem("op_done"), sem("d_ready"), sem("x_updated")
        n_mv, n_var, n_rstd, n_done, n_kept = (sem(s) for s in ("n_mv", "n_var", "n_rstd", "n_done", "n_kept"))
        xr_ready, kt_zeroed = sem("xr_ready"), sem("kt_zeroed")
        if not first:
            r_mv, r_var, r_rstd, r_norm, r_scaled = (sem(s) for s in ("r_mv", "r_var", "r_rstd", "r_norm", "r_scaled"))
            qk_mv, qk_var, qk_rstd, qk_norm, qk_scaled = (
                sem(s) for s in ("qk_mv", "qk_var", "qk_rstd", "qk_norm", "qk_scaled"))

        block = ctx.enter_context(nc.Block())

        @block.sync
        def _(sp):
            for dst, name in ((wq, "Wq"), (wk, "Wk"), (wv, "Wv"), (wo, "Wo")):
                sp.dma_start(dst[:], io[f"L{layer}_xattn_{name}"].rearrange("(c p) n -> p c n", p=P)
                             ).then_inc(w_loaded, 16)
            for r in rows:
                sp.dma_start(vec[r][:], io[f"L{layer}_xattn_{r}"].partition_broadcast(P)).then_inc(vec_loaded, 16)
            if first:
                sp.dma_start(mask[:], io["mask_1x1xSxS2_fk1"].rearrange("a b q k -> (a b q) k")
                             ).then_inc(vec_loaded, 16)
                sp.dma_start(rb[:], io["L0_ffn_router_b"].partition_broadcast(P)).then_inc(vec_loaded, 16)
            else:
                sp.dma_start(ln_s[:], io["L1_ffn_ln_scale"].partition_broadcast(P)).then_inc(vec_loaded, 16)
                sp.dma_start(ln_b[:], io["L1_ffn_ln_bias"].partition_broadcast(P)).then_inc(vec_loaded, 16)
            sp.dma_start(rw[:], moe.router.rearrange("(c p) e -> p c e", p=P)).then_inc(w_loaded, 16)

            def body(t, p):
                if not within(t, 0, nt):
                    return
                wait(sp, t1_done, t - 1)
                sp.dma_start(ctx_sb[:, p, :], io["ctx_1024"][t]).then_inc(ctx_loaded[p], 16)
                if before is not None:
                    wait(sp, z_added, t - 1)
                    sp.dma_start(zin[:, p], before[t]).then_inc(z_loaded[p], 16)
                zero_slots(t * 2, 2)
                if isinstance(t, int) and t == 1:
                    if first:
                        for c in range(1, 4):
                            load_x(core, io, sp, c)
                    zero_slots(2 * nt, moe.tiles - 2 * nt)
                if isinstance(t, int) and 1 <= t <= 3:
                    load_experts(core, moe, sp, t - 1)

            def zero_slots(s, n):
                sp.dma_start(core.slots_in[layer][bass.ds(s * P, n * P), :].rearrange("(s p) d -> p s d", p=P),
                             core.zeros[:].unsqueeze(1).broadcast_to([P, n, ROW])).then_inc(core.zeroed[layer], 16)
            over_tiles(sp, nt, body)

        nvec = 16 * (len(rows) + 2)

        @block.gpsimd
        def _(pool):
            pool.memset(qpad[:], 0.0).then_inc(init, 1)
            pool.memset(vsb[:], 1.0).then_inc(init, 1)
            pool.memset(kT[:], 0.0).then_inc(kt_zeroed, 1)
            if not first:
                pool.wait_ge(vec_loaded, nvec)

            def x_std(t, p):
                pool.wait_ge(x_mv, t + 1)
                pool.tensor_tensor(xrs[:, p, 0:1], xmv[:, p, 1:2], core.eps[:], ALU.add).then_inc(x_var, 1)
                pool.wait_ge(x_var, t + 1)
                pool.tensor_tensor(xrs[:, p, 1:2], xrs[:, p, 0:1], core.minus_half[:, 0:1],
                                   ALU.pow).then_inc(x_rstd, 1)

            def shift(t, p):
                for j in range(NJ):
                    pool.wait_ge(mx_ready, 4 * t + j + 1)
                    s = SM[:, p, j, :].rearrange("p (h k) -> p h k", h=4)
                    m = mx[:, p, 4 * j:4 * j + 4].unsqueeze(2).broadcast_to([P, 4, P])
                    pool.tensor_tensor(s, s, m, ALU.subtract).then_inc(shifted, 1)

            def qk_std(t):
                pool.wait_ge(qk_mv, t + 1)
                pool.tensor_tensor(qkrs[:, 0, :], qkmv[:, :, 1], core.eps[:].broadcast_to([P, 2]), ALU.add).then_inc(qk_var, 1)
                pool.wait_ge(qk_var, t + 1)
                pool.tensor_tensor(qkrs[:, 1, :], qkrs[:, 0, :], core.minus_half[:, 0:2],
                                   ALU.pow).then_inc(qk_rstd, 1)

            def qk_affine(t):
                pool.wait_ge(qk_norm, 2 * (t + 1))
                pool.tensor_tensor(qkn[:, 0, :], qkn[:, 0, :], vec["q_gamma"][:], ALU.mult).then_inc(qk_scaled, 1)
                pool.tensor_tensor(qkn[:, 1, :], qkn[:, 1, :], vec["k_gamma"][:], ALU.mult).then_inc(qk_scaled, 1)
                wait(pool, qt_done, t)
                wait(pool, kt_done, t)
                pool.wait_ge(qk_scaled, 2 * t + 1)
                pool.wait_ge(init, 2)
                for r in range(PAR):
                    pool.tensor_tensor(q_odd_even[:, r], as_parity(qkn[:, 0, :])[:, r],
                                       as_parity(vec["q_beta"][:])[:, r], ALU.add).then_inc(qk_ready, 1)
                pool.wait_ge(qk_scaled, 2 * t + 2)
                pool.tensor_tensor(ksb[:], qkn[:, 1, :], vec["k_beta"][:], ALU.add).then_inc(qk_ready, 1)

            def new_std(t, p):
                pool.wait_ge(n_mv, t + 1)
                wait(pool, n_kept, t - 1)
                pool.tensor_tensor(nrs[:, p:p + 1], nmv[:, p, 1:2], core.eps[:], ALU.add).then_inc(n_var, 1)
                pool.wait_ge(n_var, t + 1)
                pool.tensor_tensor(nmv[:, p, 2:3], nrs[:, p:p + 1], core.minus_half[:, 0:1],
                                   ALU.pow).then_inc(n_rstd, 1)

            def router_std(t, p):
                pool.wait_ge(r_mv, t + 1)
                pool.tensor_tensor(rrs[:, p, 0:1], rmv[:, p, 1:2], core.eps[:], ALU.add).then_inc(r_var, 1)
                pool.wait_ge(r_var, t + 1)
                pool.tensor_tensor(rrs[:, p, 1:2], rrs[:, p, 0:1], core.minus_half[:, 0:1],
                                   ALU.pow).then_inc(r_rstd, 1)

            def router_affine(t, p):
                pool.wait_ge(r_norm, t + 1)
                pool.tensor_tensor(xr[:, p, :], xr[:, p, :], ln_s[:], ALU.mult).then_inc(r_scaled, 1)
                pool.wait_ge(r_scaled, t + 1)
                pool.tensor_tensor(xr[:, p, :], xr[:, p, :], ln_b[:], ALU.add).then_inc(xr_ready, 1)

            x_std(0, 0)
            x_std(1, 1)
            if not first:
                qk_std(0)
                qk_affine(0)

            def body(i, p):
                if within(i, 0, nt - 2):
                    x_std(i + 2, p)
                if not first and within(i, 0, nt - 1):
                    qk_std(i + 1)
                if within(i, 2, nt + 2):
                    new_std(i - 2, p)
                if first:
                    if within(i, 0, nt):
                        shift(i, p)
                elif within(i, 0, nt - 1):
                    qk_affine(i + 1)
                if not first and within(i, 3, nt + 3):
                    router_affine(i - 3, 1 - p)
                if not first and within(i, 2, nt + 2):
                    router_std(i - 2, p)
            over_tiles(pool, nt, body, extra=3)

        @block.vector
        def _(dve):
            def stats_free(t):
                wait(dve, x_rstd, t - 1)
                wait(dve, xn_ready, t - 1)
                wait(dve, x_mv, t - 1)

            def add_results(t, p, count):
                stats_free(t)
                dve.wait_ge(z_loaded[p], count)
                dve.tensor_tensor(zin[:, p, 0, :], zin[:, p, 0, :], zin[:, p, 1, :], ALU.add)
                dve.drain()
                dve.tensor_tensor(X[:, t, :], X[:, t, :], zin[:, p, 0, :], ALU.add).then_inc(z_added, 1)

            def x_stats(t, p):
                if first:
                    stats_free(t)
                else:
                    dve.drain()
                dve.bn_stats(xst[:, p, :], X[:, t, :])
                dve.drain()
                dve.bn_aggr(xmv[:, p, :], xst[:, p, :]).then_inc(x_mv, 1)

            def x_norm(t, p):
                dve.wait_ge(x_rstd, t + 1)
                wait(dve, t1_done, t - 1)
                dve.tensor_scalar(xn[:, p, :], X[:, t, :], xmv[:, p, 0:1], xrs[:, p, 1:2],
                                  ALU.subtract, ALU.mult).then_inc(xn_ready, 1)

            def qk_evacuate(t):
                dve.wait_ge(qk_done, t + 1)
                wait(dve, qt_done, t)
                wait(dve, kt_done, t)
                dve.tensor_tensor(q_odd_even, as_parity(G[:, 0:D]), as_parity(vec["bq"][:]),
                                  ALU.add).then_inc(qk_ready, 1)
                dve.tensor_tensor(ksb[:], G[:, D:2 * D], vec["bk"][:], ALU.add).then_inc(qk_ready, 1)

            def qk_stats(t):
                dve.wait_ge(qk_done, t + 1)
                wait(dve, qk_mv, t)
                for a in range(2):
                    dve.bn_stats(qkst[:, a, :], G[:, a * D:(a + 1) * D])
                dve.drain()
                for a in range(2):
                    last = dve.bn_aggr(qkmv[:, a, :], qkst[:, a, :])
                last.then_inc(qk_mv, 1)

            def qk_normalise(t):
                dve.wait_ge(qk_rstd, t + 1)
                wait(dve, qk_ready, 3 * t)
                for a in range(2):
                    dve.tensor_scalar(qkn[:, a, :], G[:, a * D:(a + 1) * D], qkmv[:, a, 0:1], qkrs[:, 1, a:a + 1],
                                      ALU.subtract, ALU.mult).then_inc(qk_norm, 1)

            def v_evacuate(t, p, logits):
                dve.wait_ge(v_done, t + 1)
                if within(t, 0, nt):
                    wait(dve, av_done, 4 * (t - 1))
                    src = G[:, 0:D].rearrange("p (h w) -> p h w", h=H)
                    dst = vsb[:, p, :, 0:DH]
                    if first:
                        last = dve.tensor_tensor(dst, src, vec["bv"][:].rearrange("p (h w) -> p h w", h=H), ALU.add)
                    else:
                        last = dve.tensor_scalar(dst, src, 1.0, None, ALU.mult)
                if logits:
                    src = G[:, D:D + E]
                    if first:
                        last = dve.tensor_tensor(st["logits"][:, t - 4, :], src, rb[:], ALU.add)
                    else:
                        last = dve.tensor_scalar(st["logits"][:, t - 4, :], src, 1.0, None, ALU.mult)
                last.then_inc(v_copied, 1)

            def new_stats(t, p):
                dve.drain()
                dve.bn_stats(nst[:, p, :], X[:, t, :])
                dve.drain()
                dve.bn_aggr(nmv[:, p, 0:2], nst[:, p, :]).then_inc(n_mv, 1)

            def new_norm(t, p):
                dve.wait_ge(n_rstd, t + 1)
                if first:
                    wait(dve, kt_done, t + 3)
                else:
                    wait(dve, r_norm, t - 1)
                dst = xr if first else xn2
                dve.tensor_scalar(dst[:, p, :], X[:, t, :], nmv[:, p, 0:1], nmv[:, p, 2:3],
                                  ALU.subtract, ALU.mult).then_inc(xr_ready if first else n_done, 1)
                dve.tensor_scalar(st["norm"][:, t, :], nmv[:, p, :], 1.0, None, ALU.mult).then_inc(n_kept, 1)

            def router_stats(t, p):
                dve.wait_ge(n_done, t + 1)
                dve.bn_stats(rst[:, p, :], xn2[:, p, :])
                dve.drain()
                dve.bn_aggr(rmv[:, p, :], rst[:, p, :]).then_inc(r_mv, 1)

            def router_norm(t, p):
                dve.wait_ge(r_rstd, t + 1)
                wait(dve, kt_done, t + 3)
                dve.tensor_scalar(xr[:, p, :], xn2[:, p, :], rmv[:, p, 0:1], rrs[:, p, 1:2],
                                  ALU.subtract, ALU.mult).then_inc(r_norm, 1)

            def scores_max(t, p, between):
                by_head = lambda ap: ap.rearrange("p (h k) -> p h k", h=NJ)
                mrow = mask[:].unsqueeze(1).broadcast_to([P, NJ, P]) if first else None
                wait(dve, pt_done, 4 * (t - 1))
                wait(dve, shifted if first else s_copied, 4 * (t - 1))

                def scale(j):
                    dve.wait_ge(s_done, 4 * t + j + 1)
                    dve.scalar_tensor_tensor(out=by_head(SM[:, p, j, :]), in0=by_head(Sps[j][:]), scalar=DH ** -0.5,
                                             in1=mrow, op0=ALU.mult, op1=ALU.add).then_inc(s_copied, 1)

                def maximum(j):
                    dve.wait_ge(s_copied if first else s_done, 4 * t + j + 1)
                    dve.tensor_reduce(mx[:, p, 4 * j:4 * j + 4], by_head(SM[:, p, j, :] if first else Sps[j][:]),
                                      AX.X, ALU.max).then_inc(mx_ready, 1)

                def subtract(j):
                    dve.wait_ge(mx_ready, 4 * t + j + 1)
                    dve.tensor_tensor(by_head(SM[:, p, j, :]), by_head(Sps[j][:]),
                                      mx[:, p, 4 * j:4 * j + 4].unsqueeze(2).broadcast_to([P, NJ, P]),
                                      ALU.subtract).then_inc(s_copied, 1)

                for j in range(NJ):
                    for step in (scale, maximum) if first else (maximum, subtract):
                        step(j)
                    between(j)

            def divide(t):
                dve.wait_ge(av_done, 4 * (t + 1))
                o = O[:, 0:H * VROW].rearrange("p (h w) -> p h w", h=H)
                dve.reciprocal(rsum[:], o[:, :, DH]).then_inc(rsum_ready, 1)
                dve.wait_ge(rsum_ready, t + 1)
                wait(dve, ot_done, t)
                dve.tensor_tensor(osb[:].rearrange("p (h w) -> p h w", h=H), o[:, :, 0:DH],
                                  rsum[:].unsqueeze(2).broadcast_to([P, H, DH]), ALU.mult).then_inc(o_ready, 1)

            def update(t):
                dve.wait_ge(op_done, t + 1)
                dve.tensor_tensor(delta[:], O[:, 0:D], vec["bo"][:], ALU.add).then_inc(d_ready, 1)
                dve.wait_ge(d_ready, t + 1)
                wait(dve, n_kept, t - 1)
                dve.tensor_tensor(X[:, t, :], X[:, t, :], delta[:], ALU.add).then_inc(x_updated, 1)

            dve.wait_ge(vec_loaded, nvec)
            dve.wait_ge(init, 2)
            if first:
                dve.wait_ge(core.x_loaded[0], 16)
                dve.tensor_scalar(mask[:], mask[:], -1e9, None, ALU.mult).then_inc(init, 1)
                dve.wait_ge(init, 3)
            for t in (0, 1):
                if not first:
                    add_results(t, t, 16)
                x_stats(t, t)
            for t in (0, 1):
                x_norm(t, t)
            if first:
                qk_evacuate(0)
            else:
                qk_stats(0)
                qk_normalise(0)
            v_evacuate(0, 0, False)

            if first:
                dve.wait_ge(core.x_loaded[1], 48)

            def body(i, p):
                def between(b):
                    if b == 0 and not first and within(i, 0, nt - 1):
                        qk_normalise(i + 1)
                    if b == 1 and within(i, 0, nt - 2):
                        x_norm(i + 2, p)
                    if b == 2 and within(i, 2, nt + 2):
                        new_norm(i - 2, p)
                        if not first:
                            router_stats(i - 2, p)

                if within(i, 0, nt - 2):
                    if not first:
                        add_results(i + 2, p, 8 * i - 8 * p + 32)
                    x_stats(i + 2, p)
                if not first and within(i, 3, nt + 3):
                    router_norm(i - 3, 1 - p)
                if within(i, 0, nt - 1):
                    if first:
                        qk_evacuate(i + 1)
                    else:
                        qk_stats(i + 1)
                if within(i, 2, nt + 2):
                    update(i - 2)
                    new_stats(i - 2, p)
                if within(i, 0, nt):
                    scores_max(i, p, between)
                else:
                    for b in range(NJ):
                        between(b)
                if within(i, 1, nt + 1):
                    divide(i - 1)
                if within(i, 0, nt - 1) or within(i, 3, nt + 3):
                    v_evacuate(i + 1, 1 - p, within(i, 3, nt + 3))
            over_tiles(dve, nt, body, extra=3)

        @block.scalar
        def _(act):
            scale = 1.0 if first else D ** -0.5

            def copy(out, in_, done, count, src_free=None):
                act.activation(out, in_, ACT.Copy).then_inc(done, 1)

            def t1(t, p):
                act.wait_ge(t1_done, t + 1)
                wait(act, v_done, t - 1)
                act.copy(T1s[:, p].rearrange("p c k -> p (c k)"), T1ps[:]).then_inc(t1_copied, 1)

            def qt(t):
                act.wait_ge(qt_done, t + 1)
                act.copy(qT[:].rearrange("p c k -> p (c k)"), PTps[0][:]).then_inc(qt_copied, 1)

            def kt(t):
                act.wait_ge(kt_done, t + 1)
                if within(t, 0, nt):
                    for j in range(NJ):
                        g = slice(GRP * j, GRP * (j + 1))
                        last = act.copy(kT[g, :, j, :], PTps[1][g, 0:KC * P].rearrange("p (c k) -> p c k", c=KC))
                if within(t, 4, nt + 4):
                    last = act.copy(xrT[:].rearrange("p c k -> p (c k)"), PTps[1][:, KC * P:2 * KC * P])
                last.then_inc(kt_copied, 1)

            def pt(t, j):
                act.wait_ge(pt_done, 4 * t + j + 1)
                wait(act, av_done, 4 * t + j - 1)
                act.copy(PTs[:, j % 2, :], PTps[j % 2][:]).then_inc(pt_copied, 1)

            def ot(t):
                act.wait_ge(ot_done, t + 1)
                act.copy(oT[:].rearrange("p c k -> p (c k)"), O[:, 0:D]).then_inc(ot_copied, 1)

            def exps(t, p, j):
                act.wait_ge(shifted if first else s_copied, 4 * t + j + 1)
                act.activation(SM[:, p, j, :], SM[:, p, j, :], ACT.Exp, scale=scale).then_inc(probs, 1)

            t1(0, 0)
            qt(0)
            act.wait_ge(kt_zeroed, 1)
            kt(0)
            t1(1, 1)

            def body(i, p):
                weights, this, later = within(i, 1, nt + 1), within(i, 0, nt), within(i, 0, nt - 1)
                if weights:
                    pt(i - 1, 0)
                    pt(i - 1, 1)
                    pt(i - 1, 2)
                if this:
                    exps(i, p, 0)
                if weights:
                    pt(i - 1, 3)
                if this:
                    exps(i, p, 1)
                if later:
                    qt(i + 1)
                if this:
                    exps(i, p, 2)
                if within(i, 0, nt + 3):
                    kt(i + 1)
                if within(i, 0, nt - 2):
                    t1(i + 2, p)
                if this:
                    exps(i, p, 3)
                if weights:
                    ot(i - 1)
            over_tiles(act, nt, body, extra=3)

        @block.tensor
        def _(pe):
            def t1(t, p, count):
                pe.wait_ge(ctx_loaded[p], count)
                pe.wait_ge(xn_ready, t + 1)
                wait(pe, s_copied, 4 * t - 7)
                for c in range(KC):
                    pe.transpose(T1ps[:, c * P:(c + 1) * P], ctx_sb[:, p, c * P:(c + 1) * P], ident[:])
                for c in range(KC):
                    last = pe.transpose(T1ps[:, (KC + c) * P:(KC + c + 1) * P], xn[:, p, c * P:(c + 1) * P], ident[:])
                last.then_inc(t1_done, 1)

            def product(out, p, lhs, w):
                for c in range(KC):
                    last = pe.matmul(out, T1s[:, p, lhs * KC + c, :], w[:, c, :], start=c == 0, stop=c == KC - 1)
                return last

            def qk(t, p):
                pe.wait_ge(t1_copied, t + 1)
                wait(pe, v_copied, t)
                product(G[:, 0:D], p, 1, wq)
                product(G[:, D:2 * D], p, 0, wk).then_inc(qk_done, 1)

            def v(t, p):
                if within(t, 0, nt):
                    if first:
                        pe.wait_ge(qk_ready, 2 * (t + 1))
                    else:
                        pe.wait_ge(qk_norm, 2 * (t + 1))
                    last = product(G[:, 0:D], p, 0, wv)
                if within(t, 4, nt + 4):
                    pe.wait_ge(kt_copied, t + 1)
                    pe.wait_ge(v_copied, t)
                    for c in range(KC):
                        last = pe.matmul(G[:, D:D + E], xrT[:, c, :], rw[:, c, :], start=c == 0, stop=c == KC - 1)
                last.then_inc(v_done, 1)

            def q_transpose(t):
                wait(pe, pt_copied, 4 * t - 5)
                pe.wait_ge(qk_ready, (2 if first else 3) * (t + 1))
                for x in range(PAR * KC):
                    last = pe.transpose(PTps[0][:, x * P:(x + 1) * P], qpad[:, x * P:(x + 1) * P], ident[:])
                last.then_inc(qt_done, 1)

            def k_transpose(t, p):
                wait(pe, pt_copied, min(4 * t - 4, 4 * nt) if isinstance(t, int) else 4 * t - 4)
                if within(t, 0, nt):
                    for c in range(KC):
                        last = pe.transpose(PTps[1][:, c * P:(c + 1) * P], ksb[:, c * P:(c + 1) * P], ident[:])
                else:
                    pe.wait_ge(kt_copied, t)
                if within(t, 4, nt + 4):
                    pe.wait_ge(xr_ready, t - 3)
                    for c in range(KC):
                        last = pe.transpose(PTps[1][:, (KC + c) * P:(KC + c + 1) * P], xr[:, p, c * P:(c + 1) * P],
                                            ident[:])
                last.then_inc(kt_done, 1)

            def scores(t, b):
                c, par = divmod(b, PAR)
                pe.wait_ge(kt_copied, t + 1)
                wait(pe, s_copied, 4 * t + b - 3)
                pe.matmul(Sps[b][:], qT[:, par * KC + c, :], kT[:, c, :, :].rearrange("p j k -> p (j k)"),
                          start=True, stop=True).then_inc(s_done, 1)

            def weights_transpose(t, p, j):
                pe.wait_ge(probs, 4 * t + j + 1)
                wait(pe, pt_copied, 4 * t + j - 1)
                if j == 0:
                    pe.wait_ge(qt_copied, min(t + 2, nt) if isinstance(t, int) else t + 2)
                if j == 1:
                    pe.wait_ge(kt_copied, t + 2)
                for x in range(4):
                    last = pe.transpose(PTps[j % 2][:, x * P:(x + 1) * P], SM[:, p, j, x * P:(x + 1) * P], ident[:])
                last.then_inc(pt_done, 1)

            def weigh(t, p, j):
                pe.wait_ge(pt_copied, 4 * t + j + 1)
                for x, h in enumerate(heads_of(j)):
                    last = pe.matmul(O[:, h * VROW:(h + 1) * VROW], PTs[:, j % 2, x * P:(x + 1) * P],
                                     vsb[:, p, h, :], start=True, stop=True)
                last.then_inc(av_done, 1)

            def out_transpose(t):
                pe.wait_ge(o_ready, t + 1)
                for c in range(KC):
                    last = pe.transpose(O[:, c * P:(c + 1) * P], osb[:, c * P:(c + 1) * P], ident[:])
                last.then_inc(ot_done, 1)

            def out_product(t):
                pe.wait_ge(ot_copied, t + 1)
                for c in range(KC):
                    last = pe.matmul(O[:, 0:D], oT[:, c, :], wo[:, c, :], start=c == 0, stop=c == KC - 1)
                last.then_inc(op_done, 1)

            pe.wait_ge(w_loaded, 80)
            t1(0, 0, 16)
            qk(0, 0)
            v(0, 0)
            q_transpose(0)
            k_transpose(0, 0)
            t1(1, 1, 16)

            def body(i, p):
                q = 1 - p
                weights, this, later = within(i, 1, nt + 1), within(i, 0, nt), within(i, 0, nt - 1)
                if later:
                    qk(i + 1, q)
                if within(i, 2, nt + 2):
                    out_product(i - 2)
                for j in range(NJ):
                    if weights:
                        weights_transpose(i - 1, q, j)
                        if j == 1:
                            wait(pe, x_updated, i - 1)
                        if j >= 1:
                            weigh(i - 1, q, j - 1)
                    if this:
                        scores(i, j)
                if later:
                    q_transpose(i + 1)
                if within(i, 0, nt + 3):
                    k_transpose(i + 1, q)
                if weights:
                    weigh(i - 1, q, NJ - 1)
                if within(i, 0, nt - 2):
                    t1(i + 2, p, 8 * i - 8 * p + 32)
                if later or within(i, 3, nt + 3):
                    v(i + 1, q)
                if weights:
                    out_transpose(i - 1)
            over_tiles(pe, nt, body, extra=3)


class Moe:

    def __init__(self, layer, nt, io):
        self.layer, self.nt = layer, nt
        names = ("L0_ffn_w1", "L0_ffn_w3", "L0_ffn_w2") if layer == 0 else ("L1_ffn_Wg", "L1_ffn_Wu", "L1_ffn_Wd")
        self.gate, self.up, self.down = (io[n] for n in names)
        self.E, _, self.F = self.gate.shape
        self.units = self.F // BANK
        self.tiles = (2 * nt * P + self.E * (P - 1)) // P
        self.router = io["L0_ffn_router_w"] if layer == 0 else io["L1_ffn_gate_w"]


def load_experts(core, moe, eng, which):
    src = (moe.gate, moe.up, moe.down)[which]
    eng.dma_start(core.expert_views(moe)[which],
                  src.rearrange("e (c p) f -> p e c f", p=P)).then_inc(core.experts_loaded, 16)


def router(core, io, moe, st):
    nc = core.nc
    nt, E, S = moe.nt, moe.E, moe.tiles
    second = moe.layer == 1
    N = f"r{moe.layer}_"
    with ExitStack() as ctx:
        sem = core.phase_sems(ctx, N)
        sb = lambda name, shape, dt=F32: core.sb(N + name, shape, ctx, dt)
        upper, ones = sb("upper", [P, P]), sb("ones", [P, P])
        ints = sb("ints", [P, E + S + nt], mybir.dt.int32)
        where, past = sb("where", [P, 2, nt], mybir.dt.int32), sb("past", [P, S], mybir.dt.int32)
        idx_rev, tile_no, tok_no = sb("idx_rev", [P, E]), sb("tile_no", [P, S]), sb("tok_no", [P, nt])
        LG = st["logits"]
        big = [sb(f"big{i}", [P, nt, E]) for i in range(8)]
        PR, oh1, oh2, tmp, M, A, B, TOT = big
        small = [sb(f"small{i}", [P, nt]) for i in range(9)]
        mx, sm, m1, m2, c1, den, rden, s1, s2 = small
        cmp_cnt, cnt_t, end_a, end_b, start = sb("cmp_cnt", [P, E, nt]), sb("cnt_t", [P, E]), sb("end_a", [P, E]), sb("end_b", [P, E]), sb("start", [P, E])
        cmp_tile, eid_f = sb("cmp_tile", [P, S, E - 1]), sb("eid_f", [P, S])
        PREb, TOTb = core.bank[2], core.bank[3]

        consts, to_exp, expd, counted, prefix, chain = (sem(s) for s in ("consts", "to_exp", "expd", "counted", "prefix", "chain"))
        pool_chain = sem("pool_chain")
        block = ctx.enter_context(nc.Block())

        @block.gpsimd
        def _(pool):
            made = [0]

            def link(ins):
                made[0] += 1
                ins.then_inc(pool_chain, 1)
                pool.wait_ge(pool_chain, made[0])

            link(pool.memset(upper[:], 1.0))
            pool.affine_select(out=upper[:], in_=upper[:], compare_op=ALU.is_gt, fill=0.0, base=0,
                               pattern=[[1, P]], channel_multiplier=-1).then_inc(consts, 1)
            pool.memset(ones[:], 1.0).then_inc(consts, 1)
            link(pool.iota(ints[:, 0:E], pattern=[[-1, E]], base=E, channel_multiplier=0))
            pool.tensor_copy(idx_rev[:], ints[:, 0:E]).then_inc(consts, 1)
            link(pool.iota(ints[:, E:E + S], pattern=[[1, S]], base=0, channel_multiplier=0))
            pool.tensor_copy(tile_no[:], ints[:, E:E + S]).then_inc(consts, 1)
            link(pool.iota(ints[:, E + S:E + S + nt], pattern=[[P, nt]], base=0, channel_multiplier=0))
            pool.tensor_copy(tok_no[:], ints[:, E + S:E + S + nt]).then_inc(consts, 1)
            link(pool.iota(where[:], pattern=[[nt * P, 2], [P, nt]], base=1, channel_multiplier=1))
            pool.tensor_copy(st["meta"][:, :, :, 1].rearrange("p t w -> p w t"), where[:]).then_inc(consts, 1)
            link(pool.iota(past[:], pattern=[[P, S]], base=1 + 2 * nt * P, channel_multiplier=1))
            pool.tensor_copy(st["spare"][:], past[:]).then_inc(consts, 1)

        @block.tensor
        def _(pe):
            pe.wait_ge(consts, 7)
            pe.wait_ge(counted, 1)
            flat = M[:].rearrange("p t e -> p (t e)")
            pe.matmul(PREb[:, 0:nt * E], upper[:], flat, start=True, stop=True)
            pe.matmul(TOTb[:, 0:nt * E], ones[:], flat, start=True, stop=True).then_inc(prefix, 1)

        @block.scalar
        def _(act):
            act.wait_ge(to_exp, 1)
            act.activation(PR[:], LG[:], ACT.Exp).then_inc(expd, 1)

        @block.vector
        def _(dve):
            made = [0]

            def link(ins):
                made[0] += 1
                ins.then_inc(chain, 1)
                dve.wait_ge(chain, made[0])

            tt, red = dve.tensor_tensor, dve.tensor_reduce
            shape = [P, nt, E]
            along = lambda a: a[:].unsqueeze(2).broadcast_to(shape)
            idx = idx_rev[:].unsqueeze(1).broadcast_to(shape)
            dve.wait_ge(consts, 7)
            link(red(mx[:], LG[:], AX.X, ALU.max))
            tt(LG[:], LG[:], along(mx), ALU.subtract).then_inc(to_exp, 1)
            dve.wait_ge(expd, 1)
            link(red(sm[:], PR[:], AX.X, ALU.add))
            link(dve.reciprocal(rden[:], sm[:]))
            link(tt(PR[:], PR[:], along(rden), ALU.mult))
            link(red(m1[:], PR[:], AX.X, ALU.max))
            link(tt(tmp[:], PR[:], along(m1), ALU.is_equal))
            link(tt(tmp[:], tmp[:], idx, ALU.mult))
            link(red(c1[:], tmp[:], AX.X, ALU.max))
            link(tt(oh1[:], along(c1), idx, ALU.is_equal))
            link(dve.scalar_tensor_tensor(out=M[:], in0=oh1[:], scalar=-2.0, in1=PR[:], op0=ALU.mult, op1=ALU.add))
            link(red(m2[:], M[:], AX.X, ALU.max))
            link(tt(tmp[:], M[:], along(m2), ALU.is_equal))
            link(tt(tmp[:], tmp[:], idx, ALU.mult))
            link(red(c1[:], tmp[:], AX.X, ALU.max))
            link(tt(oh2[:], along(c1), idx, ALU.is_equal))
            tt(M[:], oh1[:], oh2[:], ALU.add).then_inc(counted, 1)
            link(tt(den[:], m1[:], m2[:], ALU.add))
            if second:
                link(dve.tensor_scalar(den[:], den[:], EPS, None, ALU.add))
            link(dve.reciprocal(rden[:], den[:]))
            link(tt(st["meta"][:, :, 0, 0], m1[:], rden[:], ALU.mult))
            link(tt(st["meta"][:, :, 1, 0], m2[:], rden[:], ALU.mult))
            dve.wait_ge(prefix, 1)
            link(dve.tensor_copy(TOT[:], TOTb[:, 0:nt * E].rearrange("p (t e) -> p t e", e=E)))
            src, dst, step = TOT, A, 1
            while step < nt:
                link(tt(dst[:, step:, :], src[:, step:, :], src[:, 0:nt - step, :], ALU.add))
                link(dve.tensor_copy(dst[:, 0:step, :], src[:, 0:step, :]))
                src, dst, step = dst, (B if dst is A else A), step * 2
            total = src
            cnt = total[:, nt - 1, :].unsqueeze(2).broadcast_to([P, E, nt])
            link(tt(cmp_cnt[:], cnt, tok_no[:].unsqueeze(1).broadcast_to([P, E, nt]), ALU.is_gt))
            link(red(cnt_t[:], cmp_cnt[:], AX.X, ALU.add))
            a, b, step = cnt_t, end_a, 1
            while step < E:
                link(tt(b[:, step:], a[:, step:], a[:, 0:E - step], ALU.add))
                link(dve.tensor_copy(b[:, 0:step], a[:, 0:step]))
                a, b, step = b, (end_b if b is end_a else end_a), step * 2
            end = a
            link(tt(cmp_tile[:], tile_no[:].unsqueeze(2).broadcast_to([P, S, E - 1]),
                    end[:, 0:E - 1].unsqueeze(1).broadcast_to([P, S, E - 1]), ALU.is_ge))
            link(red(eid_f[:], cmp_tile[:], AX.X, ALU.add))
            link(dve.tensor_copy(st["expert"][:], eid_f[:]))
            link(tt(start[:], end[:], cnt_t[:], ALU.subtract))
            link(dve.tensor_scalar(start[:], start[:], float(P), None, ALU.mult))
            link(tt(tmp[:], total[:], TOT[:], ALU.subtract))
            link(tt(tmp[:], tmp[:], start[:].unsqueeze(1).broadcast_to(shape), ALU.add))
            link(tt(tmp[:], PREb[:, 0:nt * E].rearrange("p (t e) -> p t e", e=E), tmp[:], ALU.add))
            for which, oh in enumerate((oh1, oh2)):
                link(tt(M[:], tmp[:], oh[:], ALU.mult))
                link(red((s1, s2)[which][:], M[:], AX.X, ALU.add))
                link(dve.tensor_copy(st["slot"][:, which, :], (s1, s2)[which][:]))


def scatter(moe, st, pool, rows, ready, sent):
    pool.wait_ge(st["zeroed"], 16 * (moe.nt + 1))
    for t in range(moe.nt):
        slot = t % len(sent)
        pool.wait_ge(ready, t + 1)
        for which in range(2):
            pool.indirect_dma_start(out=st["xs"], out_offset=bass.IndirectOffsetOnAxis(
                ap=st["slot"][:, which, t:t + 1], axis=0), in_=rows[:, slot, which, :], in_offset=None).then_inc(sent[slot], 16)
    for s in range(len(sent)):
        pool.wait_ge(sent[s], 32 * (moe.nt // len(sent)))


def slot_rows(dve, core, moe, st, dst, t):
    for which in range(2):
        dve.tensor_scalar(dst[:, which, 0:D], core.X[:, t, :], st["norm"][:, t, 0:1], st["norm"][:, t, 2:3],
                          ALU.subtract, ALU.mult)
    return dve.tensor_scalar(dst[:, :, D:ROW], st["meta"][:, t, :, :], 1.0, None, ALU.mult)


def ffn(core, io, moe, st, routed):
    nc = core.nc
    n = moe.tiles if routed else moe.nt
    U = moe.units
    N = f"f{moe.layer}{'r' if routed else 's'}_"
    X, ident = core.X, core.ident
    with ExitStack() as ctx:
        sem = core.phase_sems(ctx, N)
        sb = lambda name, shape: core.sb(N + name, shape, ctx)
        xin = sb("xin", [P, 2, 1, D] if routed else [P, 2, 2, ROW])
        xT = sb("xT", [P, 2, KC, P])
        sg, hid, hidT = sb("sg", [P, 2, BANK]), sb("hid", [P, 2, BANK]), sb("hidT", [P, 2, BANK])
        y = sb("y", [P, 2, D])
        if routed:
            meta, spare, index = sb("meta", [P, n, 2]), sb("spare", [P, n]), core.sb(N + "index", [P, n], ctx, mybir.dt.int32)
            meta_loaded, index_ready = sem("meta_loaded"), sem("index_ready")
        else:
            wg, wu = sb("wg", [P, KC, moe.F]), sb("wu", [P, KC, moe.F])
            wd = sb("wd", [P, moe.F // P, D])

        def ring(p, u):
            return u if U == 2 else p

        Gb, Ub, HTb = core.bank[0:2], core.bank[2:4], core.bank[4:6]
        Yb, XTb = core.bank[6], core.bank[7]

        x_in = [sem("x_in0"), sem("x_in1")]
        w_loaded, x_ready, xt_done, xt_copied = sem("w_loaded"), sem("x_ready"), sem("xt_done"), sem("xt_copied")
        g_done, u_done, silu_done, hid_ready, ht_done, ht_copied, half_done = (
            sem(s) for s in ("g_done", "u_done", "silu_done", "hid_ready", "ht_done", "ht_copied", "half_done"))
        y_done, y_copied = sem("y_done"), sem("y_copied")
        sent = [sem("sent0"), sem("sent1")]
        stored = [sem("stored0"), sem("stored1")]

        block = ctx.enter_context(nc.Block())

        @block.sync
        def _(sp):
            if not routed:
                for dst, name in ((wg, "sWg"), (wu, "sWu"), (wd, "sWd")):
                    sp.dma_start(dst[:], io[f"L1_ffn_{name}"].rearrange("(c p) f -> p c f", p=P)).then_inc(w_loaded, 16)
                return

            def body(i, p):
                if within(i, 0, n):
                    wait(sp, xt_done, i - 1)
                    sp.dma_start(xin[:, p, 0, :], st["xs"][bass.ds(i * P, P), 0:D]).then_inc(x_in[p], 16)
                if isinstance(i, int) and i == 1:
                    sp.dma_start(meta[:], st["xs"][:, D:ROW].rearrange("(s p) m -> p s m", p=P)).then_inc(meta_loaded, 16)
            over_tiles(sp, n, body)

        @block.gpsimd
        def _(pool):
            if not routed:
                scatter(moe, st, pool, xin, x_ready, sent)
                return
            pool.wait_ge(index_ready, 1)
            for i in range(n):
                pool.wait_ge(y_copied, i + 1)
                pool.indirect_dma_start(out=st["z"], out_offset=bass.IndirectOffsetOnAxis(
                    ap=index[:, i:i + 1], axis=0), in_=y[:, i % 2, :], in_offset=None).then_inc(stored[i % 2], 16)
            pool.wait_ge(stored[0], 16 * ((n + 1) // 2))
            pool.wait_ge(stored[1], 16 * (n // 2))

        @block.tensor
        def _(pe):
            pe.wait_ge(core.experts_loaded, 48 * (moe.layer + 1))
            if not routed:
                pe.wait_ge(w_loaded, 48)

            def weights(i):
                if not routed:
                    return wg, wu, wd
                e = pe.value_load(st["expert"][0:1, bass.ds(i, 1)], min_val=0, max_val=moe.E - 1)
                return tuple(v[:, bass.ds(e, 1)].squeeze(1) for v in core.expert_views(moe))

            def x_transpose(i, p, count):
                if routed:
                    pe.wait_ge(x_in[p], count)
                else:
                    pe.wait_ge(x_ready, i + 1)
                wait(pe, xt_copied, i)
                for c in range(KC):
                    last = pe.transpose(XTb[:, c * P:(c + 1) * P], xin[:, p, 0, c * P:(c + 1) * P], ident[:])
                last.then_inc(xt_done, 1)

            def product(bank, i, p, u, w):
                for c in range(KC):
                    last = pe.matmul(bank[:], xT[:, p, c, :], w[:, c, u * BANK:(u + 1) * BANK],
                                     start=c == 0, stop=c == KC - 1)
                return last

            def gate(i, p, u, w):
                k, r = i * U + u, ring(p, u)
                pe.wait_ge(xt_copied, i + 1)
                wait(pe, silu_done, k - 1)
                product(Gb[r], i, p, u, w[0]).then_inc(g_done, 1)

            def up(i, p, u, w):
                k, r = i * U + u, ring(p, u)
                wait(pe, hid_ready, k - 1)
                product(Ub[r], i, p, u, w[1]).then_inc(u_done, 1)

            def hid_transpose(i, p, u):
                k, r = i * U + u, ring(p, u)
                pe.wait_ge(hid_ready, k + 1)
                wait(pe, ht_copied, k - 1)
                for c in range(4):
                    last = pe.transpose(HTb[r][:, c * P:(c + 1) * P], hid[:, r, c * P:(c + 1) * P], ident[:])
                last.then_inc(ht_done, 1)

            def down(i, p, u, w):
                k, r = i * U + u, ring(p, u)
                pe.wait_ge(ht_copied, k + 1)
                if u == 0:
                    wait(pe, y_copied, i)
                for c in range(4):
                    last = pe.matmul(Yb[:, 0:D], hidT[:, r, c * P:(c + 1) * P], w[2][:, u * 4 + c, :],
                                     start=u == 0 and c == 0, stop=u == U - 1 and c == 3)
                last.then_inc(y_done if u == U - 1 else half_done, 1)

            x_transpose(0, 0, 16)

            def body(i, p):
                w_now = weights(i) if within(i, 0, n) else None
                for u in range(U):
                    prev = (i, p, u - 1) if u else (i - 1, 1 - p, U - 1)
                    there = within(i, 0, n) if u else within(i, 1, n + 1)
                    if within(i, 0, n):
                        gate(i, p, u, w_now)
                    if there:
                        hid_transpose(*prev)
                    if u == 0 and within(i, 0, n - 1):
                        x_transpose(i + 1, 1 - p, 8 * i + 8 * p + 16)
                    if within(i, 0, n):
                        up(i, p, u, w_now)
                    if there:
                        down(*prev, w_now if u else weights(i - 1))
            over_tiles(pe, n, body)

        @block.scalar
        def _(act):
            def xt(i, p):
                act.wait_ge(xt_done, i + 1)
                wait(act, u_done, (i - 1) * U)
                act.copy(xT[:, p].rearrange("p c k -> p (c k)"), XTb[:, 0:D]).then_inc(xt_copied, 1)

            def silu(i, p, u):
                k, r = i * U + u, ring(p, u)
                act.wait_ge(g_done, k + 1)
                wait(act, hid_ready, k - 1)
                act.activation(sg[:, r, :], Gb[r][:], ACT.Silu).then_inc(silu_done, 1)

            def ht(i, p, u):
                k, r = i * U + u, ring(p, u)
                act.wait_ge(ht_done, k + 1)
                act.copy(hidT[:, r, :], HTb[r][:]).then_inc(ht_copied, 1)

            xt(0, 0)

            def body(i, p):
                for u in range(U):
                    if within(i, 0, n):
                        silu(i, p, u)
                    if u == 0:
                        if within(i, 1, n + 1):
                            ht(i - 1, 1 - p, U - 1)
                        if within(i, 0, n - 1):
                            xt(i + 1, 1 - p)
                    elif within(i, 0, n):
                        ht(i, p, u - 1)
            over_tiles(act, n, body)

        @block.vector
        def _(dve):
            def normalise(i, p):
                wait(dve, xt_done, i - 1)
                wait(dve, sent[p], 16 * (i - p))
                slot_rows(dve, core, moe, st, xin[:, p], i).then_inc(x_ready, 1)

            def multiply(i, p, u):
                k, r = i * U + u, ring(p, u)
                dve.wait_ge(silu_done, k + 1)
                dve.wait_ge(u_done, k + 1)
                wait(dve, ht_done, k - 1)
                dve.tensor_tensor(hid[:, r, :], Ub[r][:], sg[:, r, :], ALU.mult).then_inc(hid_ready, 1)

            def places():
                dve.wait_ge(meta_loaded, 16)
                dve.scalar_tensor_tensor(out=spare[:], in0=meta[:, :, 1], scalar=0.0, in1=st["spare"][:],
                                         op0=ALU.is_equal, op1=ALU.mult)
                dve.drain()
                dve.tensor_tensor(spare[:], spare[:], meta[:, :, 1], ALU.add)
                dve.drain()
                dve.tensor_copy(index[:], spare[:]).then_inc(index_ready, 1)

            def result(i, p, stores):
                dve.wait_ge(y_done, i + 1)
                if routed:
                    wait(dve, stored[p], stores)
                    dve.tensor_scalar(y[:, p, :], Yb[:, 0:D], meta[:, bass.ds(i, 1), 0], None,
                                      ALU.mult).then_inc(y_copied, 1)
                else:
                    dve.tensor_tensor(X[:, i, :], Yb[:, 0:D], X[:, i, :], ALU.add).then_inc(y_copied, 1)

            if not routed:
                normalise(0, 0)

            def body(i, p):
                if not routed and within(i, 0, n - 1):
                    normalise(i + 1, 1 - p)
                for u in range(U):
                    if within(i, 0, n):
                        multiply(i, p, u)
                    if u == 0 and within(i, 1, n + 1):
                        if routed and isinstance(i, int) and i == 1:
                            places()
                        result(i - 1, 1 - p, 8 * (i - 2 + p))
            over_tiles(dve, n, body)


def dispatch(core, moe, st):
    N, R = f"d{moe.layer}_", 4
    with ExitStack() as ctx:
        sem = core.phase_sems(ctx, N)
        rows = core.sb(N + "rows", [P, R, 2, ROW], ctx)
        ready, sent = sem("ready"), [sem(f"sent{r}") for r in range(R)]
        block = ctx.enter_context(core.nc.Block())

        @block.vector
        def _(dve):
            def normalise(t, r, turn):
                wait(dve, sent[r], 32 * turn)
                slot_rows(dve, core, moe, st, rows[:, r], t).then_inc(ready, 1)
            for r in range(R):
                normalise(r, r, 0)
            with dve.Fori(1, moe.nt // R) as turn:
                for r in range(R):
                    normalise(turn * R + r, r, turn)

        @block.gpsimd
        def _(pool):
            scatter(moe, st, pool, rows, ready, sent)


def layer(core, io, moe):
    with ExitStack() as ctx:
        sb = lambda name, shape, dt=F32: core.sb(f"m{moe.layer}_{name}", shape, ctx, dt)
        st = {
            "norm": sb("norm", [P, moe.nt, 3]),
            "logits": sb("logits", [P, moe.nt, moe.E]),
            "meta": sb("meta", [P, moe.nt, 2, 2]),
            "spare": sb("spare", [P, moe.tiles]), "slot": sb("slot", [P, 2, moe.nt], mybir.dt.int32),
            "expert": sb("expert", [P, moe.tiles], mybir.dt.int32),
            "xs": core.slots_in[moe.layer], "z": core.results[moe.layer], "zeroed": core.zeroed[moe.layer],
        }
        attention(core, io, moe.layer, moe.nt, moe, st)
        router(core, io, moe, st)
        if moe.layer == 0:
            dispatch(core, moe, st)
        else:
            ffn(core, io, moe, st, routed=False)
        ffn(core, io, moe, st, routed=True)


def finish(core, moe, out):
    nt, T = moe.nt, 4
    results = core.results[moe.layer][1:1 + 2 * nt * P, :].rearrange("(w t p) d -> w p t d", w=2, p=P)
    Z = core.W[:, 0:2, 0:nt * D].rearrange("p w (t d) -> p w t d", d=D)
    loaded = [core.sem(f"results_loaded{c}") for c in range(nt // T)]
    summed, added, stored = core.sem("results_summed"), core.sem("results_added"), core.sem("stored")
    with core.nc.Block() as block:

        @block.sync
        def _(sp):
            for c in range(nt // T):
                for w in range(2):
                    sp.dma_start(Z[:, w, c * T:(c + 1) * T], results[w][:, c * T:(c + 1) * T]).then_inc(loaded[c], 16)

        @block.vector
        def _(dve):
            for c in range(nt // T):
                part = slice(c * T, (c + 1) * T)
                dve.wait_ge(loaded[c], 32)
                dve.tensor_tensor(Z[:, 0, part], Z[:, 0, part], Z[:, 1, part], ALU.add).then_inc(summed, 1)
                dve.wait_ge(summed, c + 1)
                dve.tensor_tensor(core.X[:, part], core.X[:, part], Z[:, 0, part], ALU.add).then_inc(added, 1)

        @block.scalar
        def _(act):
            for c in range(nt // T):
                part = slice(c * T, (c + 1) * T)
                act.wait_ge(added, c + 1)
                act.dma_start(out[part].rearrange("t p d -> p t d"), core.X[:, part, :]).then_inc(stored, 16)
            act.wait_ge(stored, 16 * (nt // T))


def build(nc, io, out):
    nt = io["x"].shape[0]
    with ExitStack() as stack:
        core = Core(nc, stack)
        core.X = core.sb("X", [P, nt, D])
        core.ident = core.sb("ident", [P, P])
        core.minus_half = core.sb("minus_half", [P, nt])
        core.eps = core.sb("eps", [P, 1])
        core.zeros = core.sb("zeros", [P, ROW])
        moes = [Moe(layer, nt, io) for layer in range(2)]
        size = max(m.E * m.F * KC for m in moes)
        core.W = core.sb("W", [P, 3, size])
        core.slots_in = [nc.dram_tensor(f"slots_in{m.layer}", (m.tiles * P, ROW), F32).ap() for m in moes]
        core.results = [nc.dram_tensor(f"results{m.layer}", (1 + 2 * nt * P + m.tiles * P, D), F32).ap() for m in moes]
        core.zeroed = [core.sem(f"slots_zeroed{m.layer}") for m in moes]
        core.x_loaded = [core.sem("x_first_loaded"), core.sem("x_rest_loaded")]
        core.experts_loaded = core.sem("experts_loaded")
        core.bank = [stack.enter_context(nc.psum_tensor(f"bank{b}", [P, BANK], F32)) for b in range(8)]
        load_constants(core, io)
        layer(core, io, moes[0])
        layer(core, io, moes[1])
        finish(core, moes[1], out)


def kernel(**inputs):
    import numpy as np
    import concourse.bacc as bacc
    from concourse.bass_utils import run_bass_kernel_spmd

    nc = bacc.Bacc("TRN2", target_bir_lowering=False, num_devices=1)
    arrays, io = {}, {}
    for name, value in inputs.items():
        a = np.ascontiguousarray(np.asarray(value).T if name == "L1_ffn_gate_w" else np.asarray(value))
        arrays[name] = a
        io[name] = nc.dram_tensor(name, a.shape, mybir.dt.from_np(a.dtype), kind="ExternalInput").ap()
    out = nc.dram_tensor("out", inputs["x"].shape, F32, kind="ExternalOutput").ap()
    build(nc, io, out)
    result = run_bass_kernel_spmd(nc, [arrays], core_ids=[0])
    return result.results[0]["out"]
```

```python
from contextlib import ExitStack

import concourse.bass as bass
from concourse import mybir

F32 = mybir.dt.float32
F32R = mybir.dt.float32r
ALU = mybir.AluOpType
ACT = mybir.ActivationFunctionType
AX = mybir.AxisListType

P = 128
D = 256
KC = D // P
H = 16
DH = D // H
EPS = 1e-5
GRP = 32
PAR = 2
NJ = P // GRP
QROW = D + DH
VROW = DH + 1
BANK = 512
ROW = D + 2


def wait(eng, sem, value):
    if isinstance(value, int) and value <= 0:
        return
    eng.wait_ge(sem, value)


def over_tiles(eng, n, body, extra=1):
    first, turns = 4, n // 2 - 1
    for i in range(first):
        body(i, i % 2)
    with eng.Fori(first // 2, turns) as turn:
        for p in (0, 1):
            body(2 * turn + p, p)
    for i in range(2 * turns, n + extra):
        body(i, i % 2)


def rest(dve, out, whole, high):
    return dve.tensor_tensor(out, whole, high.bitcast(F32), ALU.subtract)


def within(i, low, high):
    return not isinstance(i, int) or low <= i < high


class Core:

    def __init__(self, nc, stack):
        self.nc, self.stack = nc, stack

    def expert_views(self, moe):
        n = moe.E * moe.F * KC
        g, u = (self.W[:, a, 0:n].rearrange("p (e c f) -> p e c f", e=moe.E, c=KC) for a in (0, 1))
        return g, u, self.W[:, 2, 0:n].rearrange("p (e c d) -> p e c d", e=moe.E, d=D)

    def results_of(self, layer):
        rows = 2 * self.X.shape[1] * P
        return self.results[layer][1:1 + rows, :].rearrange("(w t p) d -> t p w d", w=2, p=P)

    def phase_sems(self, ctx, prefix):
        taken = []

        def clear():
            with self.nc.Block() as block:

                @block.gpsimd
                def _(pool):
                    for s in taken:
                        pool.sem_clear(s)

        def sem(name):
            taken.append(sems.enter_context(self.nc.semaphore(prefix + name)))
            return taken[-1]

        sems = ctx.enter_context(ExitStack())
        ctx.callback(clear)
        return sem

    def sem(self, name):
        return self.stack.enter_context(self.nc.semaphore(name))

    def sb(self, name, shape, stack=None, dt=F32):
        return (stack or self.stack).enter_context(self.nc.sbuf_tensor(name, shape, dt))


def load_x(core, io, eng, c):
    n = core.X.shape[1] // 4
    part = slice(c * n, (c + 1) * n)
    eng.dma_start(core.X[:, part, :], io["x"][part].rearrange("t p d -> p t d")).then_inc(core.x_loaded[min(c, 1)], 16)


def load_constants(core, io):
    nc = core.nc
    zeroed, ready = core.sem("ident_zeroed"), core.sem("constants_ready")
    with nc.Block() as block:

        @block.sync
        def _(sp):
            load_x(core, io, sp, 0)

        @block.gpsimd
        def _(pool):
            pool.memset(core.ident[:], 0.0).then_inc(zeroed, 1)
            pool.wait_ge(zeroed, 1)
            pool.affine_select(out=core.ident[:], in_=core.ident[:], compare_op=ALU.not_equal, fill=1.0,
                               base=0, pattern=[[-1, P]], channel_multiplier=1).then_inc(ready, 1)
            pool.memset(core.minus_half[:], -0.5).then_inc(ready, 1)
            pool.memset(core.eps[:], EPS).then_inc(ready, 1)
            pool.memset(core.zeros[:], 0.0).then_inc(ready, 1)
            pool.wait_ge(ready, 4)


def attention(core, io, layer, nt, moe, st):
    E = moe.E
    nc = core.nc
    first = layer == 0
    N = f"a{layer}_"
    X, ident = core.X, core.ident
    with ExitStack() as ctx:
        sem = core.phase_sems(ctx, N)
        sb = lambda name, shape, dt=F32: core.sb(N + name, shape, ctx, dt)
        split = lambda name, shape: (sb(name + "_high", shape, F32R), sb(name + "_low", shape, F32R))
        wq, wk, wv = (split(w, [P, KC, D]) for w in ("wq", "wk", "wv"))
        wo = sb("wo", [P, KC, D])
        rows = ["bq", "bk", "bv", "bo"] if first else ["bo", "q_gamma", "q_beta", "k_gamma", "k_beta"]
        vec = {r: sb(r, [P, D]) for r in rows}
        ctx_sb = sb("ctx", [P, 2, D])
        xn = sb("xn", [P, 2, D])
        T1s = split("ctxT_xnT", [P, 2, 4, P])
        qpad = sb("qpad", [P, PAR * QROW])
        qkn = None if first else sb("qkn", [P, 2, D])
        ksb = sb("ksb", [P, D]) if first else qkn[:, 1, :]
        vsb = sb("vsb", [P, 2, H, VROW])
        qT = sb("qT", [P, PAR * KC, P])
        kT = sb("kT", [P, KC, NJ, P])
        xrT = sb("routerT", [P, KC, P])
        SM = sb("scores", [P, 2, NJ, BANK])
        raw = [SM[:, 0, w, :].rearrange("p (c d) -> p c d", c=KC) for w in range(3)]
        mx = sb("mx", [P, 2, H])
        PTs = sb("weightsT", [P, 2, BANK])
        rsum = sb("rsum", [P, H])
        osb = sb("osb", [P, D])
        oT = sb("oT", [P, KC, P])
        xst, xmv, xrs = sb("xst", [P, 2, 6]), sb("xmv", [P, 2, 2]), sb("xrs", [P, 2, 2])
        nst, nmv, nrs = sb("nst", [P, 2, 6]), sb("nmv", [P, 2, 3]), sb("nrs", [P, 2])
        xr = sb("xr", [P, 2, D])
        rw = sb("rw", [P, KC, E])
        if first:
            mask = sb("mask", [P, P])
            rb = sb("rb", [P, E])
        else:
            before = core.results_of(layer - 1)
            zin = sb("zin", [P, 2, D])
            z_loaded, z_added = sem("z_loaded"), sem("z_added")
            xn2, rst, rmv, rrs = sb("xn2", [P, 2, D]), sb("rst", [P, 2, 6]), sb("rmv", [P, 2, 2]), sb("rrs", [P, 2, 2])
            ln_s, ln_b = sb("ln_s", [P, D]), sb("ln_b", [P, D])
            qkst, qkmv, qkrs = sb("qkst", [P, 2, 6]), sb("qkmv", [P, 2, 2]), sb("qkrs", [P, 2, 2])

        Sps = [core.bank[j] for j in range(NJ)]
        PTps = [core.bank[4], core.bank[5]]
        G, O = core.bank[6], core.bank[7]
        T1ps = core.bank[0]

        def heads_of(b):
            c, par = divmod(b, PAR)
            return [(c * NJ + j) * PAR + par for j in range(NJ)]

        q_odd_even = qpad[:].rearrange("p (r w) -> p r w", r=PAR)[:, :, 0:D].rearrange(
            "p r (m w) -> p r m w", w=PAR * DH)[:, :, :, 0:DH]

        def as_parity(ap):
            return ap.rearrange("p (m r w) -> p r m w", r=PAR, w=DH)

        w_loaded, vec_loaded, init = sem("w_loaded"), sem("vec_loaded"), sem("buffers_set")
        ctx_loaded = [sem("ctx_loaded0"), sem("ctx_loaded1")]
        x_mv, x_var, x_rstd, xn_ready = (sem(s) for s in ("x_mv", "x_var", "x_rstd", "xn_ready"))
        w_high, w_split = sem("w_high"), sem("w_split")
        t1_done, t1_high, t1_split = sem("t1_done"), sem("t1_high"), sem("t1_split")
        qk_done, qk_copied, qk_ready = sem("qk_done"), sem("qk_copied"), sem("qk_ready")
        v_done, v_copied = sem("v_done"), sem("v_copied")
        qt_done, qt_copied, kt_done, kt_copied = (sem(s) for s in ("qt_done", "qt_copied", "kt_done", "kt_copied"))
        s_done, s_copied, mx_ready, shifted, probs = (sem(s) for s in ("s_done", "s_copied", "mx_ready", "shifted", "probs"))
        pt_done, pt_copied, av_done = sem("pt_done"), sem("pt_copied"), sem("av_done")
        rsum_ready, o_ready, ot_done, ot_copied = (sem(s) for s in ("rsum_ready", "o_ready", "ot_done", "ot_copied"))
        op_done, x_updated = sem("op_done"), sem("x_updated")
        n_mv, n_var, n_rstd, n_done, n_kept = (sem(s) for s in ("n_mv", "n_var", "n_rstd", "n_done", "n_kept"))
        xr_ready, kt_zeroed, rt_copied = sem("xr_ready"), sem("kt_zeroed"), sem("rt_copied")
        if not first:
            r_mv, r_var, r_rstd, r_norm, r_scaled = (sem(s) for s in ("r_mv", "r_var", "r_rstd", "r_norm", "r_scaled"))
            qk_mv, qk_var, qk_rstd, qk_norm, qk_scaled = (
                sem(s) for s in ("qk_mv", "qk_var", "qk_rstd", "qk_norm", "qk_scaled"))

        block = ctx.enter_context(nc.Block())

        @block.sync
        def _(sp):
            def weights_and_vectors():
                for dst, name in zip(raw + [wo[:]], ("Wq", "Wk", "Wv", "Wo")):
                    sp.dma_start(dst, io[f"L{layer}_xattn_{name}"].rearrange("(c p) n -> p c n", p=P)
                                 ).then_inc(w_loaded, 16)
                for r in rows:
                    sp.dma_start(vec[r][:], io[f"L{layer}_xattn_{r}"].partition_broadcast(P)).then_inc(vec_loaded, 16)
                if first:
                    sp.dma_start(mask[:], io["mask_1x1xSxS2_fk1"].rearrange("a b q k -> (a b q) k")
                                 ).then_inc(vec_loaded, 16)
                    sp.dma_start(rb[:], io["L0_ffn_router_b"].partition_broadcast(P)).then_inc(vec_loaded, 16)
                else:
                    sp.dma_start(ln_s[:], io["L1_ffn_ln_scale"].partition_broadcast(P)).then_inc(vec_loaded, 16)
                    sp.dma_start(ln_b[:], io["L1_ffn_ln_bias"].partition_broadcast(P)).then_inc(vec_loaded, 16)
                sp.dma_start(rw[:], moe.router.rearrange("(c p) e -> p c e", p=P)).then_inc(w_loaded, 16)

            def body(t, p):
                if not within(t, 0, nt):
                    return
                wait(sp, t1_done, t - 1)
                sp.dma_start(ctx_sb[:, p, :], io["ctx_1024"][t]).then_inc(ctx_loaded[p], 16)
                if not first:
                    wait(sp, z_added, t)
                    sp.dma_start(zin[:], before[t]).then_inc(z_loaded, 16)
                if isinstance(t, int) and t == 0:
                    weights_and_vectors()
                zero_slots(t * 2, 2)
                if isinstance(t, int) and t == 1:
                    if first:
                        for c in range(1, 4):
                            load_x(core, io, sp, c)
                    zero_slots(2 * nt, moe.tiles - 2 * nt)
                if isinstance(t, int) and 1 <= t <= 3:
                    load_experts(core, moe, sp, t - 1)

            def zero_slots(s, n):
                sp.dma_start(core.slots_in[layer][bass.ds(s * P, n * P), :].rearrange("(s p) d -> p s d", p=P),
                             core.zeros[:].unsqueeze(1).broadcast_to([P, n, ROW])).then_inc(core.zeroed[layer], 16)
            over_tiles(sp, nt, body)

        nvec = 16 * (len(rows) + 2)

        @block.gpsimd
        def _(pool):
            pool.memset(qpad[:], 0.0).then_inc(init, 1)
            pool.memset(vsb[:], 1.0).then_inc(init, 1)
            pool.memset(kT[:], 0.0).then_inc(kt_zeroed, 1)

            def x_std(t, p):
                pool.wait_ge(x_mv, t + 1)
                pool.tensor_tensor(xrs[:, p, 0:1], xmv[:, p, 1:2], core.eps[:], ALU.add).then_inc(x_var, 1)
                pool.wait_ge(x_var, t + 1)
                pool.tensor_tensor(xrs[:, p, 1:2], xrs[:, p, 0:1], core.minus_half[:, 0:1],
                                   ALU.pow).then_inc(x_rstd, 1)

            def shift(t, p):
                for j in range(NJ):
                    pool.wait_ge(mx_ready, 4 * t + j + 1)
                    s = SM[:, p, j, :].rearrange("p (h k) -> p h k", h=4)
                    m = mx[:, p, 4 * j:4 * j + 4].unsqueeze(2).broadcast_to([P, 4, P])
                    pool.tensor_tensor(s, s, m, ALU.subtract).then_inc(shifted, 1)

            def qk_std(t):
                pool.wait_ge(qk_mv, t + 1)
                pool.tensor_tensor(qkrs[:, 0, :], qkmv[:, :, 1], core.eps[:].broadcast_to([P, 2]), ALU.add).then_inc(qk_var, 1)
                pool.wait_ge(qk_var, t + 1)
                pool.tensor_tensor(qkrs[:, 1, :], qkrs[:, 0, :], core.minus_half[:, 0:2],
                                   ALU.pow).then_inc(qk_rstd, 1)

            def qk_affine(t):
                pool.wait_ge(qk_norm, 2 * (t + 1))
                pool.tensor_tensor(qkn[:, 0, :], qkn[:, 0, :], vec["q_gamma"][:], ALU.mult).then_inc(qk_scaled, 1)
                pool.tensor_tensor(qkn[:, 1, :], qkn[:, 1, :], vec["k_gamma"][:], ALU.mult).then_inc(qk_scaled, 1)
                wait(pool, qt_done, t)
                wait(pool, kt_done, t)
                pool.wait_ge(qk_scaled, 2 * t + 1)
                pool.wait_ge(init, 2)
                for r in range(PAR):
                    pool.tensor_tensor(q_odd_even[:, r], as_parity(qkn[:, 0, :])[:, r],
                                       as_parity(vec["q_beta"][:])[:, r], ALU.add).then_inc(qk_ready, 1)
                pool.wait_ge(qk_scaled, 2 * t + 2)
                pool.tensor_tensor(ksb, qkn[:, 1, :], vec["k_beta"][:], ALU.add).then_inc(qk_ready, 1)

            def new_std(t, p):
                pool.wait_ge(n_mv, t + 1)
                wait(pool, n_kept, t - 1)
                pool.tensor_tensor(nrs[:, p:p + 1], nmv[:, p, 1:2], core.eps[:], ALU.add).then_inc(n_var, 1)
                pool.wait_ge(n_var, t + 1)
                pool.tensor_tensor(nmv[:, p, 2:3], nrs[:, p:p + 1], core.minus_half[:, 0:1],
                                   ALU.pow).then_inc(n_rstd, 1)

            def router_std(t, p):
                pool.wait_ge(r_mv, t + 1)
                pool.tensor_tensor(rrs[:, p, 0:1], rmv[:, p, 1:2], core.eps[:], ALU.add).then_inc(r_var, 1)
                pool.wait_ge(r_var, t + 1)
                pool.tensor_tensor(rrs[:, p, 1:2], rrs[:, p, 0:1], core.minus_half[:, 0:1],
                                   ALU.pow).then_inc(r_rstd, 1)

            def router_affine(t, p):
                pool.wait_ge(r_norm, t + 1)
                pool.tensor_tensor(xr[:, p, :], xr[:, p, :], ln_s[:], ALU.mult).then_inc(r_scaled, 1)
                pool.wait_ge(r_scaled, t + 1)
                pool.tensor_tensor(xr[:, p, :], xr[:, p, :], ln_b[:], ALU.add).then_inc(xr_ready, 1)

            x_std(0, 0)
            x_std(1, 1)
            if not first:
                pool.wait_ge(vec_loaded, nvec)
                qk_std(0)
                qk_affine(0)

            def body(i, p):
                if within(i, 0, nt - 2):
                    x_std(i + 2, p)
                if not first and within(i, 0, nt - 1):
                    qk_std(i + 1)
                if within(i, 2, nt + 2):
                    new_std(i - 2, p)
                if first:
                    if within(i, 0, nt):
                        shift(i, p)
                elif within(i, 0, nt - 1):
                    qk_affine(i + 1)
                if not first and within(i, 3, nt + 3):
                    router_affine(i - 3, 1 - p)
                if not first and within(i, 2, nt + 2):
                    router_std(i - 2, p)
            over_tiles(pool, nt, body, extra=3)

        @block.vector
        def _(dve):
            def stats_free(t):
                wait(dve, x_rstd, t - 1)
                wait(dve, xn_ready, t - 1)
                wait(dve, x_mv, t - 1)

            def add_results(t):
                stats_free(t)
                dve.wait_ge(z_loaded, 16 * (t + 1))
                dve.tensor_tensor(zin[:, 0, :], zin[:, 0, :], zin[:, 1, :], ALU.add)
                dve.drain()
                dve.tensor_tensor(X[:, t, :], X[:, t, :], zin[:, 0, :], ALU.add).then_inc(z_added, 1)

            def x_stats(t, p):
                if first:
                    stats_free(t)
                else:
                    dve.drain()
                dve.bn_stats(xst[:, p, :], X[:, t, :])
                dve.drain()
                dve.bn_aggr(xmv[:, p, :], xst[:, p, :]).then_inc(x_mv, 1)

            def x_norm(t, p):
                dve.wait_ge(x_rstd, t + 1)
                wait(dve, t1_done, t - 1)
                dve.tensor_scalar(xn[:, p, :], X[:, t, :], xmv[:, p, 0:1], xrs[:, p, 1:2],
                                  ALU.subtract, ALU.mult).then_inc(xn_ready, 1)

            def t1_low(t, p):
                dve.wait_ge(t1_high, t + 1)
                rest(dve, T1s[1][:, p].rearrange("p c k -> p (c k)"), T1ps[:],
                     T1s[0][:, p].rearrange("p c k -> p (c k)")).then_inc(t1_split, 1)

            def qk_evacuate(t):
                dve.wait_ge(qk_done, t + 1)
                wait(dve, qt_done, t)
                wait(dve, kt_done, t)
                dve.tensor_tensor(q_odd_even, as_parity(G[:, 0:D]), as_parity(vec["bq"][:]),
                                  ALU.add).then_inc(qk_ready, 1)
                dve.tensor_tensor(ksb[:], G[:, D:2 * D], vec["bk"][:], ALU.add).then_inc(qk_ready, 1)

            def qk_stats(t):
                dve.wait_ge(qk_done, t + 1)
                wait(dve, qk_mv, t)
                for a in range(2):
                    dve.bn_stats(qkst[:, a, :], G[:, a * D:(a + 1) * D])
                dve.drain()
                for a in range(2):
                    last = dve.bn_aggr(qkmv[:, a, :], qkst[:, a, :])
                last.then_inc(qk_mv, 1)

            def qk_normalise(t):
                dve.wait_ge(qk_rstd, t + 1)
                wait(dve, qk_ready, 3 * t)
                wait(dve, kt_done, t)
                for a in range(2):
                    dve.tensor_scalar(qkn[:, a, :], G[:, a * D:(a + 1) * D], qkmv[:, a, 0:1], qkrs[:, 1, a:a + 1],
                                      ALU.subtract, ALU.mult).then_inc(qk_norm, 1)

            def v_evacuate(t, p, logits):
                dve.wait_ge(v_done, t + 1)
                if within(t, 0, nt):
                    wait(dve, av_done, 4 * (t - 1))
                    src = G[:, 0:D].rearrange("p (h w) -> p h w", h=H)
                    dst = vsb[:, p, :, 0:DH]
                    if first:
                        last = dve.tensor_tensor(dst, src, vec["bv"][:].rearrange("p (h w) -> p h w", h=H), ALU.add)
                    else:
                        last = dve.tensor_scalar(dst, src, 1.0, None, ALU.mult)
                if logits:
                    src = G[:, D:D + E]
                    if first:
                        last = dve.tensor_tensor(st["logits"][:, t - 4, :], src, rb[:], ALU.add)
                    else:
                        last = dve.tensor_scalar(st["logits"][:, t - 4, :], src, 1.0, None, ALU.mult)
                last.then_inc(v_copied, 1)

            def new_stats(t, p):
                dve.drain()
                dve.bn_stats(nst[:, p, :], X[:, t, :])
                dve.drain()
                dve.bn_aggr(nmv[:, p, 0:2], nst[:, p, :]).then_inc(n_mv, 1)

            def new_norm(t, p):
                dve.wait_ge(n_rstd, t + 1)
                if first:
                    wait(dve, kt_done, t + 3)
                else:
                    wait(dve, r_norm, t - 1)
                dst = xr if first else xn2
                dve.tensor_scalar(dst[:, p, :], X[:, t, :], nmv[:, p, 0:1], nmv[:, p, 2:3],
                                  ALU.subtract, ALU.mult).then_inc(xr_ready if first else n_done, 1)
                dve.tensor_scalar(st["norm"][:, t, :], nmv[:, p, :], 1.0, None, ALU.mult).then_inc(n_kept, 1)

            def router_stats(t, p):
                dve.wait_ge(n_done, t + 1)
                dve.bn_stats(rst[:, p, :], xn2[:, p, :])
                dve.drain()
                dve.bn_aggr(rmv[:, p, :], rst[:, p, :]).then_inc(r_mv, 1)

            def router_norm(t, p):
                dve.wait_ge(r_rstd, t + 1)
                wait(dve, kt_done, t + 3)
                dve.tensor_scalar(xr[:, p, :], xn2[:, p, :], rmv[:, p, 0:1], rrs[:, p, 1:2],
                                  ALU.subtract, ALU.mult).then_inc(r_norm, 1)

            def scores_max(t, p, between):
                by_head = lambda ap: ap.rearrange("p (h k) -> p h k", h=NJ)
                mrow = mask[:].unsqueeze(1).broadcast_to([P, NJ, P]) if first else None
                wait(dve, pt_done, 4 * (t - 1))
                wait(dve, shifted if first else s_copied, 4 * (t - 1))

                def scale(j):
                    dve.wait_ge(s_done, 4 * t + j + 1)
                    dve.scalar_tensor_tensor(out=by_head(SM[:, p, j, :]), in0=by_head(Sps[j][:]), scalar=DH ** -0.5,
                                             in1=mrow, op0=ALU.mult, op1=ALU.add).then_inc(s_copied, 1)

                def maximum(j):
                    dve.wait_ge(s_copied if first else s_done, 4 * t + j + 1)
                    dve.tensor_reduce(mx[:, p, 4 * j:4 * j + 4], by_head(SM[:, p, j, :] if first else Sps[j][:]),
                                      AX.X, ALU.max).then_inc(mx_ready, 1)

                def subtract(j):
                    dve.wait_ge(mx_ready, 4 * t + j + 1)
                    dve.tensor_tensor(by_head(SM[:, p, j, :]), by_head(Sps[j][:]),
                                      mx[:, p, 4 * j:4 * j + 4].unsqueeze(2).broadcast_to([P, NJ, P]),
                                      ALU.subtract).then_inc(s_copied, 1)

                for j in range(NJ):
                    for step in (scale, maximum) if first else (maximum, subtract):
                        step(j)
                    between(j)

            def divide(t):
                dve.wait_ge(av_done, 4 * (t + 1))
                o = O[:, 0:H * VROW].rearrange("p (h w) -> p h w", h=H)
                dve.reciprocal(rsum[:], o[:, :, DH]).then_inc(rsum_ready, 1)
                dve.wait_ge(rsum_ready, t + 1)
                wait(dve, ot_done, t)
                dve.tensor_tensor(osb[:].rearrange("p (h w) -> p h w", h=H), o[:, :, 0:DH],
                                  rsum[:].unsqueeze(2).broadcast_to([P, H, DH]), ALU.mult).then_inc(o_ready, 1)

            def update(t):
                dve.wait_ge(op_done, t + 1)
                wait(dve, n_kept, t - 1)
                dve.tensor_tensor(X[:, t, :], X[:, t, :], O[:, 0:D], ALU.add).then_inc(x_updated, 1)
                dve.wait_ge(x_updated, t + 1)
                dve.tensor_tensor(X[:, t, :], X[:, t, :], vec["bo"][:], ALU.add)

            if first:
                dve.wait_ge(core.x_loaded[0], 16)
            for t in (0, 1):
                if not first:
                    add_results(t)
                x_stats(t, t)
            for t in (0, 1):
                x_norm(t, t)
            for number, (w, whole) in enumerate(zip((wq, wk, wv), raw)):
                dve.wait_ge(w_high, number + 1)
                rest(dve, w[1][:], whole, w[0][:]).then_inc(w_split, 1)
            t1_low(0, 0)
            dve.wait_ge(vec_loaded, nvec)
            dve.wait_ge(init, 2)
            if first:
                dve.tensor_scalar(mask[:], mask[:], -1e9, None, ALU.mult).then_inc(init, 1)
                dve.wait_ge(init, 3)
                qk_evacuate(0)
            else:
                qk_stats(0)
                qk_normalise(0)
            v_evacuate(0, 0, False)
            t1_low(1, 1)

            if first:
                dve.wait_ge(core.x_loaded[1], 48)

            def body(i, p):
                def between(b):
                    if b == 0 and not first and within(i, 0, nt - 1):
                        qk_normalise(i + 1)
                    if b == 1 and within(i, 0, nt - 2):
                        x_norm(i + 2, p)
                    if b == 2 and within(i, 2, nt + 2):
                        new_norm(i - 2, p)
                        if not first:
                            router_stats(i - 2, p)

                if within(i, 0, nt - 2):
                    if not first:
                        add_results(i + 2)
                    x_stats(i + 2, p)
                if not first and within(i, 3, nt + 3):
                    router_norm(i - 3, 1 - p)
                if within(i, 0, nt - 1):
                    if first:
                        qk_evacuate(i + 1)
                    else:
                        qk_stats(i + 1)
                if within(i, 2, nt + 2):
                    update(i - 2)
                    new_stats(i - 2, p)
                if within(i, 0, nt):
                    scores_max(i, p, between)
                else:
                    for b in range(NJ):
                        between(b)
                if within(i, 0, nt - 2):
                    t1_low(i + 2, p)
                if within(i, 1, nt + 1):
                    divide(i - 1)
                if within(i, 0, nt - 1) or within(i, 3, nt + 3):
                    v_evacuate(i + 1, 1 - p, within(i, 3, nt + 3))
            over_tiles(dve, nt, body, extra=3)

        @block.scalar
        def _(act):
            scale = 1.0 if first else D ** -0.5

            def t1(t, p):
                act.wait_ge(t1_done, t + 1)
                wait(act, v_done, t - 1)
                act.copy(T1s[0][:, p].rearrange("p c k -> p (c k)"), T1ps[:]).then_inc(t1_high, 1)

            def qt(t):
                act.wait_ge(qt_done, t + 1)
                act.copy(qT[:].rearrange("p c k -> p (c k)"), PTps[0][:]).then_inc(qt_copied, 1)

            def kt(t):
                act.wait_ge(kt_done, t + 1)
                if within(t, 4, nt + 4):
                    act.copy(xrT[:].rearrange("p c k -> p (c k)"), PTps[1][:, KC * P:2 * KC * P]).then_inc(rt_copied, 1)
                if within(t, 0, nt):
                    for j in range(NJ):
                        g = slice(GRP * j, GRP * (j + 1))
                        last = act.copy(kT[g, :, j, :], PTps[1][g, 0:KC * P].rearrange("p (c k) -> p c k", c=KC))
                    last.then_inc(kt_copied, 1)

            def pt(t, j):
                act.wait_ge(pt_done, 4 * t + j + 1)
                wait(act, av_done, 4 * t + j - 1)
                act.copy(PTs[:, j % 2, :], PTps[j % 2][:]).then_inc(pt_copied, 1)

            def ot(t):
                act.wait_ge(ot_done, t + 1)
                act.copy(oT[:].rearrange("p c k -> p (c k)"), O[:, 0:D]).then_inc(ot_copied, 1)

            def exps(t, p, j):
                act.wait_ge(shifted if first else s_copied, 4 * t + j + 1)
                act.activation(SM[:, p, j, :], SM[:, p, j, :], ACT.Exp, scale=scale).then_inc(probs, 1)

            act.wait_ge(w_loaded, 80)
            for w, whole in zip((wq, wk, wv), raw):
                act.copy(w[0][:], whole).then_inc(w_high, 1)
            t1(0, 0)
            qt(0)
            act.wait_ge(kt_zeroed, 1)
            kt(0)
            t1(1, 1)

            def body(i, p):
                weights, this, later = within(i, 1, nt + 1), within(i, 0, nt), within(i, 0, nt - 1)
                if weights:
                    pt(i - 1, 0)
                    pt(i - 1, 1)
                    pt(i - 1, 2)
                if this:
                    exps(i, p, 0)
                if weights:
                    pt(i - 1, 3)
                if this:
                    exps(i, p, 1)
                if within(i, 0, nt - 2):
                    t1(i + 2, p)
                if later:
                    qt(i + 1)
                if this:
                    exps(i, p, 2)
                if within(i, 0, nt + 3):
                    kt(i + 1)
                if this:
                    exps(i, p, 3)
                if weights:
                    ot(i - 1)
            over_tiles(act, nt, body, extra=3)

        @block.tensor
        def _(pe):
            def t1(t, p, count):
                pe.wait_ge(ctx_loaded[p], count)
                pe.wait_ge(xn_ready, t + 1)
                wait(pe, s_copied, 4 * t - 7)
                for c in range(KC):
                    pe.transpose(T1ps[:, c * P:(c + 1) * P], ctx_sb[:, p, c * P:(c + 1) * P], ident[:])
                for c in range(KC):
                    last = pe.transpose(T1ps[:, (KC + c) * P:(KC + c + 1) * P], xn[:, p, c * P:(c + 1) * P], ident[:])
                last.then_inc(t1_done, 1)

            def product(out, t, p, lhs, w):
                for number, (a, b) in enumerate(((0, 0), (0, 1), (1, 0))):
                    if number == 2:
                        pe.wait_ge(t1_split, t + 1)
                    for c in range(KC):
                        last = pe.matmul(out, T1s[a][:, p, lhs * KC + c, :], w[b][:, c, :],
                                         start=number == 0 and c == 0, stop=number == 2 and c == KC - 1)
                return last

            def qk(t, p):
                pe.wait_ge(t1_high, t + 1)
                wait(pe, v_copied, t)
                product(G[:, 0:D], t, p, 1, wq)
                product(G[:, D:2 * D], t, p, 0, wk).then_inc(qk_done, 1)

            def v(t, p):
                if within(t, 0, nt):
                    if first:
                        pe.wait_ge(qk_ready, 2 * (t + 1))
                    else:
                        pe.wait_ge(qk_norm, 2 * (t + 1))
                    last = product(G[:, 0:D], t, p, 0, wv)
                if within(t, 4, nt + 4):
                    pe.wait_ge(rt_copied, t - 3)
                    pe.wait_ge(v_copied, t)
                    for c in range(KC):
                        last = pe.matmul(G[:, D:D + E], xrT[:, c, :], rw[:, c, :], start=c == 0, stop=c == KC - 1)
                last.then_inc(v_done, 1)

            def q_transpose(t):
                wait(pe, pt_copied, 4 * t - 5)
                pe.wait_ge(qk_ready, (2 if first else 3) * (t + 1))
                for x in range(PAR * KC):
                    last = pe.transpose(PTps[0][:, x * P:(x + 1) * P], qpad[:, x * P:(x + 1) * P], ident[:])
                last.then_inc(qt_done, 1)

            def k_transpose(t, p):
                wait(pe, pt_copied, min(4 * t - 4, 4 * nt) if isinstance(t, int) else 4 * t - 4)
                if within(t, 0, nt):
                    for c in range(KC):
                        last = pe.transpose(PTps[1][:, c * P:(c + 1) * P], ksb[:, c * P:(c + 1) * P], ident[:])
                else:
                    pe.wait_ge(rt_copied, t - 4)
                if within(t, 4, nt + 4):
                    pe.wait_ge(xr_ready, t - 3)
                    for c in range(KC):
                        last = pe.transpose(PTps[1][:, (KC + c) * P:(KC + c + 1) * P], xr[:, p, c * P:(c + 1) * P],
                                            ident[:])
                last.then_inc(kt_done, 1)

            def scores(t, b):
                c, par = divmod(b, PAR)
                pe.wait_ge(kt_copied, t + 1)
                wait(pe, s_copied, 4 * t + b - 3)
                pe.matmul(Sps[b][:], qT[:, par * KC + c, :], kT[:, c, :, :].rearrange("p j k -> p (j k)"),
                          start=True, stop=True).then_inc(s_done, 1)

            def weights_transpose(t, p, j):
                pe.wait_ge(probs, 4 * t + j + 1)
                wait(pe, pt_copied, 4 * t + j - 1)
                if j == 0:
                    pe.wait_ge(qt_copied, min(t + 2, nt) if isinstance(t, int) else t + 2)
                if j == 1:
                    if within(t, 0, nt - 1):
                        pe.wait_ge(kt_copied, t + 2)
                    else:
                        pe.wait_ge(rt_copied, t - 2)
                for x in range(4):
                    last = pe.transpose(PTps[j % 2][:, x * P:(x + 1) * P], SM[:, p, j, x * P:(x + 1) * P], ident[:])
                last.then_inc(pt_done, 1)

            def weigh(t, p, j):
                pe.wait_ge(pt_copied, 4 * t + j + 1)
                for x, h in enumerate(heads_of(j)):
                    last = pe.matmul(O[:, h * VROW:(h + 1) * VROW], PTs[:, j % 2, x * P:(x + 1) * P],
                                     vsb[:, p, h, :], start=True, stop=True)
                last.then_inc(av_done, 1)

            def out_transpose(t):
                pe.wait_ge(o_ready, t + 1)
                for c in range(KC):
                    last = pe.transpose(O[:, c * P:(c + 1) * P], osb[:, c * P:(c + 1) * P], ident[:])
                last.then_inc(ot_done, 1)

            def out_product(t):
                pe.wait_ge(ot_copied, t + 1)
                for c in range(KC):
                    last = pe.matmul(O[:, 0:D], oT[:, c, :], wo[:, c, :], start=c == 0, stop=c == KC - 1)
                last.then_inc(op_done, 1)

            pe.wait_ge(w_loaded, 80)
            pe.wait_ge(w_split, 3)
            t1(0, 0, 16)
            qk(0, 0)
            v(0, 0)
            q_transpose(0)
            k_transpose(0, 0)
            t1(1, 1, 16)

            def body(i, p):
                q = 1 - p
                weights, this, later = within(i, 1, nt + 1), within(i, 0, nt), within(i, 0, nt - 1)
                if later:
                    qk(i + 1, q)
                if within(i, 2, nt + 2):
                    out_product(i - 2)
                for j in range(NJ):
                    if weights:
                        weights_transpose(i - 1, q, j)
                        if j == 1:
                            wait(pe, x_updated, i - 1)
                        if j >= 1:
                            weigh(i - 1, q, j - 1)
                    if this:
                        scores(i, j)
                if within(i, 0, nt - 2):
                    t1(i + 2, p, 8 * i - 8 * p + 32)
                if later:
                    q_transpose(i + 1)
                if within(i, 0, nt + 3):
                    k_transpose(i + 1, q)
                if weights:
                    weigh(i - 1, q, NJ - 1)
                if later or within(i, 3, nt + 3):
                    v(i + 1, q)
                if weights:
                    out_transpose(i - 1)
            over_tiles(pe, nt, body, extra=3)


class Moe:

    def __init__(self, layer, nt, io):
        self.layer, self.nt = layer, nt
        names = ("L0_ffn_w1", "L0_ffn_w3", "L0_ffn_w2") if layer == 0 else ("L1_ffn_Wg", "L1_ffn_Wu", "L1_ffn_Wd")
        self.gate, self.up, self.down = (io[n] for n in names)
        self.E, _, self.F = self.gate.shape
        self.units = self.F // BANK
        self.tiles = (2 * nt * P + self.E * (P - 1)) // P
        self.router = io["L0_ffn_router_w"] if layer == 0 else io["L1_ffn_gate_w"]


def load_experts(core, moe, eng, which):
    src = (moe.gate, moe.up, moe.down)[which]
    eng.dma_start(core.expert_views(moe)[which],
                  src.rearrange("e (c p) f -> p e c f", p=P)).then_inc(core.experts_loaded, 16)


def router(core, io, moe, st):
    nc = core.nc
    nt, E, S = moe.nt, moe.E, moe.tiles
    second = moe.layer == 1
    N = f"r{moe.layer}_"
    with ExitStack() as ctx:
        sem = core.phase_sems(ctx, N)
        sb = lambda name, shape, dt=F32: core.sb(N + name, shape, ctx, dt)
        upper, ones = sb("upper", [P, P]), sb("ones", [P, P])
        ints = sb("ints", [P, E + S + nt], mybir.dt.int32)
        where, past = sb("where", [P, 2, nt], mybir.dt.int32), sb("past", [P, S], mybir.dt.int32)
        idx_rev, tile_no, tok_no = sb("idx_rev", [P, E]), sb("tile_no", [P, S]), sb("tok_no", [P, nt])
        LG = st["logits"]
        big = [sb(f"big{i}", [P, nt, E]) for i in range(8)]
        PR, oh1, oh2, tmp, M, A, B, TOT = big
        small = [sb(f"small{i}", [P, nt]) for i in range(9)]
        mx, sm, m1, m2, c1, den, rden, s1, s2 = small
        cmp_cnt, cnt_t, end_a, end_b, start = sb("cmp_cnt", [P, E, nt]), sb("cnt_t", [P, E]), sb("end_a", [P, E]), sb("end_b", [P, E]), sb("start", [P, E])
        cmp_tile, eid_f = sb("cmp_tile", [P, S, E - 1]), sb("eid_f", [P, S])
        PREb, TOTb = core.bank[2], core.bank[3]

        consts, to_exp, expd, counted, prefix, chain = (sem(s) for s in ("consts", "to_exp", "expd", "counted", "prefix", "chain"))
        pool_chain = sem("pool_chain")
        block = ctx.enter_context(nc.Block())

        @block.gpsimd
        def _(pool):
            made = [0]

            def link(ins):
                made[0] += 1
                ins.then_inc(pool_chain, 1)
                pool.wait_ge(pool_chain, made[0])

            link(pool.memset(upper[:], 1.0))
            pool.affine_select(out=upper[:], in_=upper[:], compare_op=ALU.is_gt, fill=0.0, base=0,
                               pattern=[[1, P]], channel_multiplier=-1).then_inc(consts, 1)
            pool.memset(ones[:], 1.0).then_inc(consts, 1)
            link(pool.iota(ints[:, 0:E], pattern=[[-1, E]], base=E, channel_multiplier=0))
            pool.tensor_copy(idx_rev[:], ints[:, 0:E]).then_inc(consts, 1)
            link(pool.iota(ints[:, E:E + S], pattern=[[1, S]], base=0, channel_multiplier=0))
            pool.tensor_copy(tile_no[:], ints[:, E:E + S]).then_inc(consts, 1)
            link(pool.iota(ints[:, E + S:E + S + nt], pattern=[[P, nt]], base=0, channel_multiplier=0))
            pool.tensor_copy(tok_no[:], ints[:, E + S:E + S + nt]).then_inc(consts, 1)
            link(pool.iota(where[:], pattern=[[nt * P, 2], [P, nt]], base=1, channel_multiplier=1))
            pool.tensor_copy(st["meta"][:, :, :, 1].rearrange("p t w -> p w t"), where[:]).then_inc(consts, 1)
            link(pool.iota(past[:], pattern=[[P, S]], base=1 + 2 * nt * P, channel_multiplier=1))
            pool.tensor_copy(st["spare"][:], past[:]).then_inc(consts, 1)

        @block.tensor
        def _(pe):
            pe.wait_ge(consts, 7)
            pe.wait_ge(counted, 1)
            flat = M[:].rearrange("p t e -> p (t e)")
            pe.matmul(PREb[:, 0:nt * E], upper[:], flat, start=True, stop=True)
            pe.matmul(TOTb[:, 0:nt * E], ones[:], flat, start=True, stop=True).then_inc(prefix, 1)

        @block.scalar
        def _(act):
            act.wait_ge(to_exp, 1)
            act.activation(PR[:], LG[:], ACT.Exp).then_inc(expd, 1)

        @block.vector
        def _(dve):
            made = [0]

            def link(ins):
                made[0] += 1
                ins.then_inc(chain, 1)
                dve.wait_ge(chain, made[0])

            tt, red = dve.tensor_tensor, dve.tensor_reduce
            shape = [P, nt, E]
            along = lambda a: a[:].unsqueeze(2).broadcast_to(shape)
            idx = idx_rev[:].unsqueeze(1).broadcast_to(shape)
            dve.wait_ge(consts, 7)
            link(red(mx[:], LG[:], AX.X, ALU.max))
            tt(LG[:], LG[:], along(mx), ALU.subtract).then_inc(to_exp, 1)
            dve.wait_ge(expd, 1)
            link(red(sm[:], PR[:], AX.X, ALU.add))
            link(dve.reciprocal(rden[:], sm[:]))
            link(tt(PR[:], PR[:], along(rden), ALU.mult))
            link(red(m1[:], PR[:], AX.X, ALU.max))
            link(tt(tmp[:], PR[:], along(m1), ALU.is_equal))
            link(tt(tmp[:], tmp[:], idx, ALU.mult))
            link(red(c1[:], tmp[:], AX.X, ALU.max))
            link(tt(oh1[:], along(c1), idx, ALU.is_equal))
            link(dve.scalar_tensor_tensor(out=M[:], in0=oh1[:], scalar=-2.0, in1=PR[:], op0=ALU.mult, op1=ALU.add))
            link(red(m2[:], M[:], AX.X, ALU.max))
            link(tt(tmp[:], M[:], along(m2), ALU.is_equal))
            link(tt(tmp[:], tmp[:], idx, ALU.mult))
            link(red(c1[:], tmp[:], AX.X, ALU.max))
            link(tt(oh2[:], along(c1), idx, ALU.is_equal))
            tt(M[:], oh1[:], oh2[:], ALU.add).then_inc(counted, 1)
            link(tt(den[:], m1[:], m2[:], ALU.add))
            if second:
                link(dve.tensor_scalar(den[:], den[:], EPS, None, ALU.add))
            link(dve.reciprocal(rden[:], den[:]))
            link(tt(st["meta"][:, :, 0, 0], m1[:], rden[:], ALU.mult))
            link(tt(st["meta"][:, :, 1, 0], m2[:], rden[:], ALU.mult))
            dve.wait_ge(prefix, 1)
            link(dve.tensor_copy(TOT[:], TOTb[:, 0:nt * E].rearrange("p (t e) -> p t e", e=E)))
            src, dst, step = TOT, A, 1
            while step < nt:
                link(tt(dst[:, step:, :], src[:, step:, :], src[:, 0:nt - step, :], ALU.add))
                link(dve.tensor_copy(dst[:, 0:step, :], src[:, 0:step, :]))
                src, dst, step = dst, (B if dst is A else A), step * 2
            total = src
            cnt = total[:, nt - 1, :].unsqueeze(2).broadcast_to([P, E, nt])
            link(tt(cmp_cnt[:], cnt, tok_no[:].unsqueeze(1).broadcast_to([P, E, nt]), ALU.is_gt))
            link(red(cnt_t[:], cmp_cnt[:], AX.X, ALU.add))
            a, b, step = cnt_t, end_a, 1
            while step < E:
                link(tt(b[:, step:], a[:, step:], a[:, 0:E - step], ALU.add))
                link(dve.tensor_copy(b[:, 0:step], a[:, 0:step]))
                a, b, step = b, (end_b if b is end_a else end_a), step * 2
            end = a
            link(tt(cmp_tile[:], tile_no[:].unsqueeze(2).broadcast_to([P, S, E - 1]),
                    end[:, 0:E - 1].unsqueeze(1).broadcast_to([P, S, E - 1]), ALU.is_ge))
            link(red(eid_f[:], cmp_tile[:], AX.X, ALU.add))
            link(dve.tensor_copy(st["expert"][:], eid_f[:]))
            link(tt(start[:], end[:], cnt_t[:], ALU.subtract))
            link(dve.tensor_scalar(start[:], start[:], float(P), None, ALU.mult))
            link(tt(tmp[:], total[:], TOT[:], ALU.subtract))
            link(tt(tmp[:], tmp[:], start[:].unsqueeze(1).broadcast_to(shape), ALU.add))
            link(tt(tmp[:], PREb[:, 0:nt * E].rearrange("p (t e) -> p t e", e=E), tmp[:], ALU.add))
            for which, oh in enumerate((oh1, oh2)):
                link(tt(M[:], tmp[:], oh[:], ALU.mult))
                link(red((s1, s2)[which][:], M[:], AX.X, ALU.add))
                link(dve.tensor_copy(st["slot"][:, which, :], (s1, s2)[which][:]))


def scatter(moe, st, pool, rows, ready, sent):
    pool.wait_ge(st["zeroed"], 16 * (moe.nt + 1))
    for t in range(moe.nt):
        slot = t % len(sent)
        pool.wait_ge(ready, t + 1)
        for which in range(2):
            pool.indirect_dma_start(out=st["xs"], out_offset=bass.IndirectOffsetOnAxis(
                ap=st["slot"][:, which, t:t + 1], axis=0), in_=rows[:, slot, which, :], in_offset=None).then_inc(sent[slot], 16)
    for s in range(len(sent)):
        pool.wait_ge(sent[s], 32 * (moe.nt // len(sent)))


def slot_rows(dve, core, moe, st, dst, t):
    for which in range(2):
        dve.tensor_scalar(dst[:, which, 0:D], core.X[:, t, :], st["norm"][:, t, 0:1], st["norm"][:, t, 2:3],
                          ALU.subtract, ALU.mult)
    return dve.tensor_scalar(dst[:, :, D:ROW], st["meta"][:, t, :, :], 1.0, None, ALU.mult)


def experts(core, io, moe, st, routed):
    nc, U = core.nc, moe.units
    n = moe.tiles if routed else moe.nt
    N = f"f{moe.layer}{'r' if routed else 's'}_"
    X, ident = core.X, core.ident
    with ExitStack() as ctx:
        sem = core.phase_sems(ctx, N)
        sb = lambda name, shape, dt=F32: core.sb(N + name, shape, ctx, dt)
        split = lambda name, shape: (sb(name + "_high", shape, F32R), sb(name + "_low", shape, F32R))
        xin = sb("xin", [P, 2, 1, D] if routed else [P, 2, 2, ROW])
        xT = split("xT", [P, 2, KC * P])
        wg, wu = split("wg", [P, 2, KC, BANK]), split("wu", [P, KC, BANK])
        wd = split("wd", [P, 2, 4, D])
        sg, hid, hT = sb("sg", [P, 2, BANK]), sb("hid", [P, BANK]), split("hT", [P, BANK])
        y, tick, tock = sb("y", [P, 2, D]), sb("tick", [P, 3]), sb("tock", [P, 2])
        if routed:
            meta, place = sb("meta", [P, n, 2]), sb("place", [P, n])
            index = sb("index", [P, 2], mybir.dt.int32)
        else:
            shared = [sb("shared_gate", [P, KC, BANK]), sb("shared_up", [P, KC, BANK]), sb("shared_down", [P, 4, D])]

        def ring(p, u):
            return u if U == 2 else p

        def piece(which, u, e):
            if not routed:
                return shared[which][:]
            w = core.expert_views(moe)[which][:, bass.ds(e, 1)].squeeze(1)
            return w[:, 4 * u:4 * u + 4, :] if which == 2 else w[:, :, u * BANK:(u + 1) * BANK]

        Gb, Ub, HTb = core.bank[0:2], core.bank[2:4], core.bank[4:6]
        Yb, XTb = core.bank[6], core.bank[7]

        if routed:
            x_in, meta_loaded = [sem("x_in0"), sem("x_in1")], sem("meta_loaded")
            stored = [sem("stored0"), sem("stored1")]
        else:
            x_ready, shared_loaded, sent = sem("x_ready"), sem("shared_loaded"), [sem("sent0"), sem("sent1")]
        xt_done, xt_high, xt_split = sem("xt_done"), sem("xt_high"), sem("xt_split")
        w_high = [sem("wg_high"), sem("wu_high"), sem("wd_high")]
        w_split = [sem("wg_split"), sem("wu_split"), sem("wd_split")]
        g_done, u_done, d_done = sem("g_done"), sem("u_done"), sem("d_done")
        silu_done, hid_ready, ht_done, ht_high, ht_split = (
            sem(s) for s in ("silu_done", "hid_ready", "ht_done", "ht_high", "ht_split"))
        y_ready = sem("y_ready")

        block = ctx.enter_context(nc.Block())

        @block.sync
        def _(sp):
            if not routed:
                for dst, name in zip(shared, ("sWg", "sWu", "sWd")):
                    sp.dma_start(dst[:], io[f"L1_ffn_{name}"].rearrange("(c p) f -> p c f", p=P)).then_inc(shared_loaded, 16)
                return

            def body(i, p):
                if within(i, 0, n):
                    wait(sp, xt_done, i - 1)
                    sp.dma_start(xin[:, p, 0, :], st["xs"][bass.ds(i * P, P), 0:D]).then_inc(x_in[p], 16)
                if isinstance(i, int) and i == 1:
                    sp.dma_start(meta[:], st["xs"][:, D:ROW].rearrange("(s p) m -> p s m", p=P)).then_inc(meta_loaded, 16)
            over_tiles(sp, n, body)

        @block.tensor
        def _(pe):
            def x_transpose(i, p, count):
                if routed:
                    pe.wait_ge(x_in[p], count)
                else:
                    pe.wait_ge(x_ready, i + 1)
                wait(pe, xt_split, i)
                for c in range(KC):
                    last = pe.transpose(XTb[:, c * P:(c + 1) * P], xin[:, p, 0, c * P:(c + 1) * P], ident[:])
                last.then_inc(xt_done, 1)

            def product(out, lhs, w, chunks, start, stop, passes):
                for number, (a, b, waits) in enumerate(passes):
                    for sem, count in waits:
                        pe.wait_ge(sem, count)
                    for c in range(chunks):
                        last = pe.matmul(out, lhs(a, c), w[b][:, c, :], start=start and number == 0 and c == 0,
                                         stop=stop and number == 2 and c == chunks - 1)
                return last

            def weights_there(parts, which, k):
                return [(parts[which], k + 1)] if routed else []

            def of_x(p):
                return lambda part, c: xT[part][:, p, c * P:(c + 1) * P]

            def gate(i, p, u):
                k, r = i * U + u, ring(p, u)
                wait(pe, silu_done, k - 1)
                product(Gb[r][:], of_x(p), [part[:, r if routed else 0] for part in wg], KC, True, True, (
                    (0, 0, [(xt_high, i + 1)] + weights_there(w_high, 0, k)),
                    (1, 0, [(xt_split, i + 1)]),
                    (0, 1, weights_there(w_split, 0, k)))).then_inc(g_done, 1)

            def up(i, p, u):
                k, r = i * U + u, ring(p, u)
                wait(pe, hid_ready, k - 1)
                product(Ub[r][:], of_x(p), wu, KC, True, True, (
                    (0, 0, weights_there(w_high, 1, k)),
                    (1, 0, []),
                    (0, 1, weights_there(w_split, 1, k)))).then_inc(u_done, 1)

            def hid_transpose(i, p, u):
                k, r = i * U + u, ring(p, u)
                pe.wait_ge(hid_ready, k + 1)
                wait(pe, ht_split, k - 1)
                for c in range(4):
                    last = pe.transpose(HTb[r][:, c * P:(c + 1) * P], hid[:, c * P:(c + 1) * P], ident[:])
                last.then_inc(ht_done, 1)

            def down(i, p, u):
                k = i * U + u
                if u == 0:
                    wait(pe, y_ready, i)
                w = [part[:, ring(p, u) if routed else 0] for part in wd]
                product(Yb[:, 0:D], lambda part, c: hT[part][:, c * P:(c + 1) * P], w, 4,
                        u == 0, u == U - 1, (
                            (0, 0, [(ht_high, k + 1)] + weights_there(w_high, 2, k)),
                            (0, 1, weights_there(w_split, 2, k)),
                            (1, 0, [(ht_split, k + 1)]))).then_inc(d_done, 1)

            x_transpose(0, 0, 16)
            if not routed:
                for which in range(3):
                    pe.wait_ge(w_split[which], 1)

            def body(i, p):
                for u in range(U):
                    prev = (i, p, u - 1) if u else (i - 1, 1 - p, U - 1)
                    there = within(i, 0, n) if u else within(i, 1, n + 1)
                    if within(i, 0, n):
                        gate(i, p, u)
                    if there:
                        hid_transpose(*prev)
                    if u == 0 and within(i, 0, n - 1):
                        x_transpose(i + 1, 1 - p, 8 * i + 8 * p + 16)
                    if within(i, 0, n):
                        up(i, p, u)
                    if there:
                        down(*prev)
            over_tiles(pe, n, body)

        @block.scalar
        def _(act):
            expert = lambda i: act.value_load(st["expert"][0:1, bass.ds(i, 1)], min_val=0, max_val=moe.E - 1)

            def silu(i, p, u):
                k, r = i * U + u, ring(p, u)
                act.wait_ge(g_done, k + 1)
                wait(act, hid_ready, k - 1)
                act.activation(sg[:, r, :], Gb[r][:], ACT.Silu).then_inc(silu_done, 1)

            def xt(i, p):
                act.wait_ge(xt_done, i + 1)
                wait(act, u_done, (i - 1) * U)
                act.copy(xT[0][:, p, :], XTb[:, 0:D]).then_inc(xt_high, 1)

            def ht(i, p, u):
                k, r = i * U + u, ring(p, u)
                act.wait_ge(ht_done, k + 1)
                act.copy(hT[0][:], HTb[r][:]).then_inc(ht_high, 1)

            def high(which, k, u, e, slot=None):
                used = k if which == 1 else k - 1
                if which > 0 and within(used, 1, n * U):
                    act.wait_ge((g_done, u_done, d_done)[which], used)
                    mark = 2 if which == 1 else slot
                    act.copy(tick[:, mark:mark + 1], core.eps[:])
                out = wu[0][:] if which == 1 else (wg if which == 0 else wd)[0][:, slot]
                act.copy(out, piece(which, u, e)).then_inc(w_high[which], 1)

            if routed:
                act.wait_ge(core.experts_loaded, 48 * (moe.layer + 1))
                first = expert(0)
            else:
                act.wait_ge(shared_loaded, 48)
                first = None
            high(0, 0, 0, first, 0)
            xt(0, 0)
            high(1, 0, 0, first)
            if not routed:
                high(2, 0, 0, first, 0)

            ahead_of = [None]

            def body(i, p):
                e = ahead_of[0] if p else expert(i) if routed and within(i, 0, n) else None
                e_next = ahead_of[0] = expert(i + 1) if routed and within(i, 0, n - 1) else None
                for u in range(U):
                    k, last = i * U + u, u == U - 1
                    ahead = routed and (within(i, 0, n - 1) if last else within(i, 0, n))
                    u_next, e_of = (0, e_next) if last else (u + 1, e)
                    if ahead:
                        high(0, k + 1, u_next, e_of, 1 - ring(p, u))
                    if within(i, 0, n):
                        silu(i, p, u)
                    if u and within(i, 0, n):
                        ht(i, p, u - 1)
                    if u == 0 and within(i, 1, n + 1):
                        ht(i - 1, 1 - p, U - 1)
                    if u == 0 and within(i, 0, n - 1):
                        xt(i + 1, 1 - p)
                    if routed and within(i, 0, n):
                        high(2, k, u, e, ring(p, u))
                    if ahead:
                        high(1, k + 1, u_next, e_of)
            over_tiles(act, n, body)

        @block.vector
        def _(dve):
            expert = lambda i: dve.value_load(st["expert"][0:1, bass.ds(i, 1)], min_val=0, max_val=moe.E - 1)

            def low(which, k, u, e, slot=None):
                dve.wait_ge(w_high[which], k + 1)
                high, out = [w[:] if which == 1 else w[:, slot] for w in (wg, wu, wd)[which]]
                rest(dve, out, piece(which, u, e), high).then_inc(w_split[which], 1)

            def normalise(i, p):
                wait(dve, xt_done, i - 1)
                wait(dve, sent[p], 16 * (i - p))
                slot_rows(dve, core, moe, st, xin[:, p], i).then_inc(x_ready, 1)

            def xt(i, p):
                dve.wait_ge(xt_high, i + 1)
                rest(dve, xT[1][:, p, :], XTb[:, 0:D], xT[0][:, p, :]).then_inc(xt_split, 1)

            def ht(i, p, u):
                k, r = i * U + u, ring(p, u)
                dve.wait_ge(ht_high, k + 1)
                rest(dve, hT[1][:], HTb[r][:], hT[0][:]).then_inc(ht_split, 1)

            def multiply(i, p, u):
                k, r = i * U + u, ring(p, u)
                dve.wait_ge(silu_done, k + 1)
                dve.wait_ge(u_done, k + 1)
                dve.tensor_tensor(hid[:], Ub[r][:], sg[:, r, :], ALU.mult).then_inc(hid_ready, 1)

            def places():
                dve.wait_ge(meta_loaded, 16)
                dve.scalar_tensor_tensor(out=place[:], in0=meta[:, :, 1], scalar=0.0, in1=st["spare"][:],
                                         op0=ALU.is_equal, op1=ALU.mult)
                dve.drain()
                dve.tensor_tensor(place[:], place[:], meta[:, :, 1], ALU.add)
                dve.drain()

            def result(i, p, stores):
                dve.wait_ge(d_done, (i + 1) * U)
                if not routed:
                    dve.tensor_tensor(X[:, i, :], Yb[:, 0:D], X[:, i, :], ALU.add).then_inc(y_ready, 1)
                    return
                wait(dve, stored[p], stores)
                dve.tensor_scalar(y[:, p, :], Yb[:, 0:D], meta[:, bass.ds(i, 1), 0], None, ALU.mult)
                dve.tensor_copy(index[:, p:p + 1], place[:, bass.ds(i, 1)]).then_inc(y_ready, 1)

            if routed:
                dve.wait_ge(core.experts_loaded, 48 * (moe.layer + 1))
                first = expert(0)
            else:
                normalise(0, 0)
                dve.wait_ge(shared_loaded, 48)
                first = None
            low(0, 0, 0, first, 0)
            xt(0, 0)
            low(1, 0, 0, first)
            if not routed:
                low(2, 0, 0, first, 0)

            ahead_of = [None]

            def body(i, p):
                e = ahead_of[0] if p or U == 1 else expert(i) if within(i, 0, n) else None
                e_next = ahead_of[0] = expert(i + 1) if routed and within(i, 0, n - 1) else None
                if not routed and within(i, 0, n - 1):
                    normalise(i + 1, 1 - p)
                for u in range(U):
                    k, last = i * U + u, u == U - 1
                    ahead = routed and (within(i, 0, n - 1) if last else within(i, 0, n))
                    u_next, e_of = (0, e_next) if last else (u + 1, e)
                    if ahead:
                        low(0, k + 1, u_next, e_of, 1 - ring(p, u))
                    if u == 0:
                        if within(i, 1, n + 1):
                            ht(i - 1, 1 - p, U - 1)
                        if within(i, 0, n - 1):
                            xt(i + 1, 1 - p)
                    elif within(i, 0, n):
                        ht(i, p, u - 1)
                    if within(i, 0, n):
                        multiply(i, p, u)
                    if ahead:
                        low(1, k + 1, u_next, e_of)
                    if u == 0 and within(i, 1, n + 1):
                        if routed and isinstance(i, int) and i == 1:
                            places()
                        result(i - 1, 1 - p, 8 * (i - 2 + p))
            over_tiles(dve, n, body)

        @block.gpsimd
        def _(pool):
            if not routed:
                scatter(moe, st, pool, xin, x_ready, sent)
                return
            expert = lambda i: pool.value_load(st["expert"][0:1, bass.ds(i, 1)], min_val=0, max_val=moe.E - 1)

            def low(k, u, e, slot):
                pool.wait_ge(w_high[2], k + 1)
                pool.tensor_tensor(tock[:, slot:slot + 1], core.eps[:], core.eps[:], ALU.add)
                pool.tensor_tensor(wd[1][:, slot], piece(2, u, e), wd[0][:, slot].bitcast(F32),
                                   ALU.subtract).then_inc(w_split[2], 1)

            def leave(p):
                pool.indirect_dma_start(out=st["z"], out_offset=bass.IndirectOffsetOnAxis(
                    ap=index[:, p:p + 1], axis=0), in_=y[:, p, :], in_offset=None).then_inc(stored[p], 16)

            def body(i, p):
                e = expert(i) if within(i, 0, n) else None
                if within(i, 2, n + 2):
                    pool.wait_ge(y_ready, i - 1)
                for u in range(U):
                    if within(i, 0, n):
                        low(i * U + u, u, e, ring(p, u))
                    if u == 0 and within(i, 2, n + 2):
                        leave(p)
            over_tiles(pool, n, body, extra=2)
            pool.wait_ge(stored[0], 16 * ((n + 1) // 2))
            pool.wait_ge(stored[1], 16 * (n // 2))


def dispatch(core, moe, st):
    N, R = f"d{moe.layer}_", 4
    with ExitStack() as ctx:
        sem = core.phase_sems(ctx, N)
        rows = core.sb(N + "rows", [P, R, 2, ROW], ctx)
        ready, sent = sem("ready"), [sem(f"sent{r}") for r in range(R)]
        block = ctx.enter_context(core.nc.Block())

        @block.vector
        def _(dve):
            def normalise(t, r, turn):
                wait(dve, sent[r], 32 * turn)
                slot_rows(dve, core, moe, st, rows[:, r], t).then_inc(ready, 1)
            for r in range(R):
                normalise(r, r, 0)
            with dve.Fori(1, moe.nt // R) as turn:
                for r in range(R):
                    normalise(turn * R + r, r, turn)

        @block.gpsimd
        def _(pool):
            scatter(moe, st, pool, rows, ready, sent)


def layer(core, io, moe):
    with ExitStack() as ctx:
        sb = lambda name, shape, dt=F32: core.sb(f"m{moe.layer}_{name}", shape, ctx, dt)
        st = {
            "norm": sb("norm", [P, moe.nt, 3]),
            "logits": sb("logits", [P, moe.nt, moe.E]),
            "meta": sb("meta", [P, moe.nt, 2, 2]),
            "spare": sb("spare", [P, moe.tiles]), "slot": sb("slot", [P, 2, moe.nt], mybir.dt.int32),
            "expert": sb("expert", [P, moe.tiles], mybir.dt.int32),
            "xs": core.slots_in[moe.layer], "z": core.results[moe.layer], "zeroed": core.zeroed[moe.layer],
        }
        attention(core, io, moe.layer, moe.nt, moe, st)
        router(core, io, moe, st)
        if moe.layer == 0:
            dispatch(core, moe, st)
        else:
            experts(core, io, moe, st, routed=False)
        experts(core, io, moe, st, routed=True)


def finish(core, moe, out):
    nt, T = moe.nt, 4
    results = core.results[moe.layer][1:1 + 2 * nt * P, :].rearrange("(w t p) d -> w p t d", w=2, p=P)
    Z = core.W[:, 0:2, 0:nt * D].rearrange("p w (t d) -> p w t d", d=D)
    loaded = [core.sem(f"results_loaded{c}") for c in range(nt // T)]
    summed, added, stored = core.sem("results_summed"), core.sem("results_added"), core.sem("stored")
    with core.nc.Block() as block:

        @block.sync
        def _(sp):
            for c in range(nt // T):
                for w in range(2):
                    sp.dma_start(Z[:, w, c * T:(c + 1) * T], results[w][:, c * T:(c + 1) * T]).then_inc(loaded[c], 16)

        @block.vector
        def _(dve):
            for c in range(nt // T):
                part = slice(c * T, (c + 1) * T)
                dve.wait_ge(loaded[c], 32)
                dve.tensor_tensor(Z[:, 0, part], Z[:, 0, part], Z[:, 1, part], ALU.add).then_inc(summed, 1)
                dve.wait_ge(summed, c + 1)
                dve.tensor_tensor(core.X[:, part], core.X[:, part], Z[:, 0, part], ALU.add).then_inc(added, 1)

        @block.scalar
        def _(act):
            for c in range(nt // T):
                part = slice(c * T, (c + 1) * T)
                act.wait_ge(added, c + 1)
                act.dma_start(out[part].rearrange("t p d -> p t d"), core.X[:, part, :]).then_inc(stored, 16)
            act.wait_ge(stored, 16 * (nt // T))


def build(nc, io, out):
    nt = io["x"].shape[0]
    with ExitStack() as stack:
        core = Core(nc, stack)
        core.X = core.sb("X", [P, nt, D])
        core.ident = core.sb("ident", [P, P])
        core.minus_half = core.sb("minus_half", [P, nt])
        core.eps = core.sb("eps", [P, 1])
        core.zeros = core.sb("zeros", [P, ROW])
        moes = [Moe(layer, nt, io) for layer in range(2)]
        size = max(m.E * m.F * KC for m in moes)
        core.W = core.sb("W", [P, 3, size])
        core.slots_in = [nc.dram_tensor(f"slots_in{m.layer}", (m.tiles * P, ROW), F32).ap() for m in moes]
        core.results = [nc.dram_tensor(f"results{m.layer}", (1 + 2 * nt * P + m.tiles * P, D), F32).ap() for m in moes]
        core.zeroed = [core.sem(f"slots_zeroed{m.layer}") for m in moes]
        core.x_loaded = [core.sem("x_first_loaded"), core.sem("x_rest_loaded")]
        core.experts_loaded = core.sem("experts_loaded")
        core.bank = [stack.enter_context(nc.psum_tensor(f"bank{b}", [P, BANK], F32)) for b in range(8)]
        load_constants(core, io)
        layer(core, io, moes[0])
        layer(core, io, moes[1])
        finish(core, moes[1], out)


def kernel(**inputs):
    import numpy as np
    import concourse.bacc as bacc
    from concourse.bass_utils import run_bass_kernel_spmd

    nc = bacc.Bacc("TRN2", target_bir_lowering=False, num_devices=1)
    arrays, io = {}, {}
    for name, value in inputs.items():
        a = np.ascontiguousarray(np.asarray(value).T if name == "L1_ffn_gate_w" else np.asarray(value))
        arrays[name] = a
        io[name] = nc.dram_tensor(name, a.shape, mybir.dt.from_np(a.dtype), kind="ExternalInput").ap()
    out = nc.dram_tensor("out", inputs["x"].shape, F32, kind="ExternalOutput").ap()
    build(nc, io, out)
    result = run_bass_kernel_spmd(nc, [arrays], core_ids=[0])
    return result.results[0]["out"]
```
